# Optimizing a Trainium2 kernel written in Bass

```python
import numpy as np
import jax
import jax.numpy as jnp

def _softmax(x, axis=-1):
    return jax.nn.softmax(x, axis=axis)

def _gelu(x):
    return jax.nn.gelu(x, approximate=True)

def _silu(x):
    return jax.nn.silu(x)

def _sigmoid(x):
    return jax.nn.sigmoid(x)

def _layernorm(x, axis=-1, eps=1e-05):
    m = jnp.mean(x, axis=axis, keepdims=True)
    v = jnp.var(x, axis=axis, keepdims=True)
    return (x - m) / jnp.sqrt(v + eps)

def _scatter_add(tgt, idx, src, axis=0):
    return tgt.at[idx].add(src)

def _segment_sum(src, seg, n):
    return jax.ops.segment_sum(src, seg, n)
kernel_name = 'mk_xattn_seq_d1_seqx_r4_10e815'

def setup_inputs(seed: int=0):
    np.random.seed(seed)
    _w = jnp.asarray

    def _rec_inputs():
        import jax
        import jax.numpy as jnp
        _rk = jax.random.key(seed)
        x = -0.0002928 + 1 * jax.random.normal(jax.random.fold_in(_rk, 1), (32, 256, 256), jnp.float32)
        _lenS = 256 - jax.random.randint(jax.random.fold_in(_rk, 7), (32,), 0, max(1, 256 // 4) + 1, jnp.int32)
        _lenS2 = 256 - jax.random.randint(jax.random.fold_in(_rk, 8), (32,), 0, max(1, 256 // 4) + 1, jnp.int32)
        _ctx_1024P = jax.random.normal(jax.random.fold_in(_rk, 11), (32, 16, 256), jnp.float32)
        _ctx_1024c = jax.random.dirichlet(jax.random.fold_in(_rk, 511), 0.3 * jnp.ones((16,), jnp.float32), (32, 256))
        _ctx_1024t = jnp.einsum('bsk,bkd->bsd', _ctx_1024c, _ctx_1024P)
        _ctx_1024t = _ctx_1024t * jax.lax.rsqrt(jnp.mean(jnp.square(_ctx_1024t)) + 1e-12) * 0.953939
        ctx_1024 = -1.39393e-06 + 0.999914 * (_ctx_1024t + 0.3 * jax.random.normal(jax.random.fold_in(_rk, 611), (32, 256, 256), jnp.float32))
        _validS = jnp.arange(256)[None, :] < _lenS[:, None]
        _validS2 = jnp.arange(256)[None, :] < _lenS2[:, None]
        _causal = jnp.tril(jnp.ones((256, 256), dtype=bool))
        mask_BxSxS2_bk1 = jnp.broadcast_to(_validS2[:, None, :], (32, 256, 256))
        return (x, ctx_1024, mask_BxSxS2_bk1)
    x, ctx_1024, mask_BxSxS2_bk1 = _rec_inputs()

    def _L0_xattn_setup():
        import jax, jax.numpy as jnp
        import numpy as np
        B, S, D, H = (2, 512, 256, 16)
        HD = D // H
        EPS = 1e-05
        key = jax.random.key(seed)
        ks = jax.random.split(key, 9)
        q = jax.random.normal(ks[0], (B, S, D), dtype=jnp.float32)
        k = jax.random.normal(ks[1], (B, S, D), dtype=jnp.float32)
        v = jax.random.normal(ks[2], (B, S, D), dtype=jnp.float32)
        sc = 1.0 / np.sqrt(D)
        wq = jax.random.normal(ks[3], (D, D), dtype=jnp.float32) * sc
        wk = jax.random.normal(ks[4], (D, D), dtype=jnp.float32) * sc
        wv = jax.random.normal(ks[5], (D, D), dtype=jnp.float32) * sc
        wo = jax.random.normal(ks[6], (D, D), dtype=jnp.float32) * sc
        gamma = jnp.ones((D,), dtype=jnp.float32)
        beta = jnp.zeros((D,), dtype=jnp.float32)
        causal = ~jnp.tril(jnp.ones((S, S), dtype=bool))
        mask = jnp.broadcast_to(causal, (B, S, S))
        return {'q': q, 'k': k, 'v': v, 'wq': wq, 'wk': wk, 'wv': wv, 'wo': wo, 'gamma': gamma, 'beta': beta, 'mask': mask}
    _L0_xattn_all = _L0_xattn_setup()
    _L0_xattn_in = {k: v for k, v in _L0_xattn_all.items() if k in ('wq', 'wk', 'wv', 'wo', 'gamma', 'beta')}
    del _L0_xattn_all
    return {'x': x, 'ctx_1024': ctx_1024, 'mask_BxSxS2_bk1': mask_BxSxS2_bk1, 'L0_xattn_wq': _L0_xattn_in['wq'], 'L0_xattn_wk': _L0_xattn_in['wk'], 'L0_xattn_wv': _L0_xattn_in['wv'], 'L0_xattn_wo': _L0_xattn_in['wo'], 'L0_xattn_gamma': _L0_xattn_in['gamma'], 'L0_xattn_beta': _L0_xattn_in['beta']}

def reference(x, ctx_1024, mask_BxSxS2_bk1, L0_xattn_wq, L0_xattn_wk, L0_xattn_wv, L0_xattn_wo, L0_xattn_gamma, L0_xattn_beta):
    import jax
    import jax.numpy as jnp

    def _L0_xattn_ref(q, k, v, wq, wk, wv, wo, gamma, beta, mask):
        import jax, jax.numpy as jnp
        import numpy as np
        B, S, D, H = (2, 512, 256, 16)
        HD = D // H
        EPS = 1e-05
        Bq, Lq, _ = q.shape
        Lk = k.shape[1]
        qs = (q @ wq).reshape(Bq, Lq, H, HD).transpose(0, 2, 1, 3)
        ks_ = (k @ wk).reshape(Bq, Lk, H, HD).transpose(0, 2, 1, 3)
        vs = (v @ wv).reshape(Bq, Lk, H, HD).transpose(0, 2, 1, 3)
        scores = jnp.einsum('bhqd,bhkd->bhqk', qs, ks_) / jnp.sqrt(jnp.float32(HD))
        scores = jnp.where(mask[:, None, :, :], -jnp.inf, scores)
        attn_w = jax.nn.softmax(scores, axis=-1)
        attn = jnp.einsum('bhqk,bhkd->bhqd', attn_w, vs)
        attn = attn.transpose(0, 2, 1, 3).reshape(Bq, Lq, H * HD)
        out = attn @ wo + q
        mu = jnp.mean(out, axis=-1, keepdims=True)
        var = jnp.mean((out - mu) ** 2, axis=-1, keepdims=True)
        return (out - mu) / jnp.sqrt(var + EPS) * gamma + beta
    x = _L0_xattn_ref(x, ctx_1024, ctx_1024, L0_xattn_wq, L0_xattn_wk, L0_xattn_wv, L0_xattn_wo, L0_xattn_gamma, L0_xattn_beta, mask_BxSxS2_bk1)
    return x

_drawn_inputs = setup_inputs


def setup_inputs(seed=0):
    import zlib

    import numpy as np

    out = dict(_drawn_inputs(seed))
    spreads = {'L0_xattn_gamma': (1.0, 0.2), 'L0_xattn_beta': (0.0, 0.1)}
    factors = {}
    for name, (base, spread) in spreads.items():
        noise = np.random.default_rng([zlib.crc32(name.encode()), seed]).standard_normal(out[name].shape)
        drawn = base * np.exp(spread * noise) if base else spread * noise
        out[name] = jnp.asarray(drawn.astype(out[name].dtype))
    for name, factor in factors.items():
        out[name] = (out[name] * factor).astype(out[name].dtype)
    return out
```

```python
import concourse.bass as bass
from concourse import mybir
from contextlib import ExitStack

F32 = mybir.dt.float32
F32R = mybir.dt.float32r
BF16 = mybir.dt.bfloat16
U8 = mybir.dt.uint8
ACT = mybir.ActivationFunctionType
ALU = mybir.AluOpType
AX = mybir.AxisListType

P = 128
BIG = 2.0 ** 100
EPS = 1e-5
N_CONST = 17
UNROLL = 4


class Batch:

    def __init__(self, t, c):
        self.t, self.c = t, c
        self.n = c if isinstance(t, int) and t == 0 else t * UNROLL + c
        self.ring = c % UNROLL
        self.side = c % 2
        self.round = c // UNROLL if isinstance(t, int) else t + c // UNROLL
        self.turn = c // 2 if isinstance(t, int) else t * (UNROLL // 2) + c // 2

    def __add__(self, n):
        return Batch(self.t, self.c + n)

    def __sub__(self, n):
        return Batch(self.t, self.c - n)

    def from_(self, n):
        return self.c >= n

    def exists(self, batches):
        return not isinstance(self.t, int) or self.c < batches


def build(nc, x, ctx_in, mask, wq, wk, wv, wo, gamma, beta, out):
    B, S, D = x.shape
    SK = ctx_in.shape[1]
    H, HD = 16, 16
    SCALE = float(HD) ** -0.5
    QT = S // P
    DT = D // P
    BK = 64
    KB = SK // BK
    HG = P // HD
    NG = H // HG
    NP = H // 2
    PQ = 32
    NM = BK + H

    ctx = ExitStack()
    with ctx:
        def sb(name, shape, dt=F32):
            return ctx.enter_context(nc.sbuf_tensor(name, shape, dt))

        def pb(name, shape, dt=F32):
            return ctx.enter_context(nc.psum_tensor(name, shape, dt))

        def sem(name):
            return ctx.enter_context(nc.semaphore(name))

        ident = sb("ident", [P, P])
        ident_b = sb("ident_b", [P, P], BF16)
        head_rows = sb("head_rows", [P, HG])
        spread32 = sb("spread32", [NM, NP, P])
        spread = sb("spread", [NM, NP, P], F32R)
        ones_pair = sb("ones_pair", [P, PQ])
        half_neg = sb("half_neg", [P, QT])
        neg_one = sb("neg_one", [P, QT])
        wq_sb = sb("wq_sb", [P, DT, D])
        wk_sb = sb("wk_sb", [P, DT, D])
        wv_sb = sb("wv_sb", [P, DT, D])
        wo_sb = sb("wo_sb", [P, DT, D])
        gamma_sb = sb("gamma_sb", [P, D])
        beta_sb = sb("beta_sb", [P, D])
        x_in = [sb(f"x_in{n}", [P, QT, D]) for n in range(UNROLL)]
        c_in = [sb(f"c_in{n}", [BK, KB, D]) for n in range(UNROLL)]
        m_in = [sb(f"m_in{n}", [P, QT, SK], U8) for n in range(UNROLL)]
        mask_b = [sb(f"mask_b{n}", [P, QT, SK], BF16) for n in range(2)]
        xT = sb("xT", [P, DT, S])
        cT = sb("cT", [P, DT, KB, 2, BK])
        q32 = [sb(f"q32_{n}", [P, NG, S]) for n in range(2)]
        q16 = sb("q16", [P, NG, S], BF16)
        kT = sb("kT", [P, NG, KB, BK])
        k32 = [sb(f"k32_{n}", [P, KB, NG, HG, BK]) for n in range(2)]
        k16 = sb("k16", [P, KB, NG, HG, BK], BF16)
        v_pair = [sb(f"v_pair{n}", [P, KB, NP, PQ]) for n in range(2)]
        addend = [sb(f"addend{n}", [NM, KB, S], F32R) for n in range(2)]
        row_max = sb("row_max", [P, KB, QT * H])
        all_max = sb("all_max", [P, QT * H])
        neg_max = sb("neg_max", [P, QT * H])
        probs = sb("probs", [P, NP, S])
        sums = sb("sums", [P, NG * S])
        recips = sb("recips", [P, NG * S])
        attn_raw = sb("attn_raw", [P, NG * S])
        attn = sb("attn", [P, NG * S])
        z = [sb(f"z{n}", [P, QT, D]) for n in range(2)]
        stats = sb("stats", [P, QT, 6])
        moments = [sb(f"moments{n}", [P, QT, 2]) for n in range(2)]
        var_eps = [sb(f"var_eps{n}", [P, QT]) for n in range(2)]
        rstd = [sb(f"rstd{n}", [P, QT]) for n in range(2)]
        mu_rstd = [sb(f"mu_rstd{n}", [P, QT]) for n in range(2)]
        shift = [sb(f"shift{n}", [P, QT]) for n in range(2)]
        zn = [sb(f"zn{n}", [P, QT, D]) for n in range(2)]
        zg = sb("zg", [P, QT, D])
        y = [sb(f"y{n}", [P, QT, D]) for n in range(2)]
        sc = pb("sc", [P, NP * S])
        p_x = pb("p_x", [P, 512])
        p_q = pb("p_q", [P, 512])
        p_y = pb("p_y", [P, 512])
        p_k = pb("p_k", [P, 512])
        mask_ps = p_y[:, :].bitcast(BF16)

        s_const = sem("s_const")
        s_const_r = sem("s_const_r")
        s_weights = sem("s_weights")
        s_loaded = [sem(f"s_loaded{n}") for n in range(UNROLL)]
        s_mask = sem("s_mask")
        s_x_turned = sem("s_x_turned")
        s_c_turned = sem("s_c_turned")
        s_m_turned = sem("s_m_turned")
        s_x_copied = sem("s_x_copied")
        s_c_copied = sem("s_c_copied")
        s_m_copied = sem("s_m_copied")
        s_k_proj = sem("s_k_proj")
        s_q_proj = sem("s_q_proj")
        s_v_proj = sem("s_v_proj")
        s_k_copied = sem("s_k_copied")
        s_k_spread = sem("s_k_spread")
        s_k_cast = sem("s_k_cast")
        s_q_copied = sem("s_q_copied")
        s_q_cast = sem("s_q_cast")
        s_v_copied = sem("s_v_copied")
        s_max_mm = sem("s_max_mm")
        s_max_red = sem("s_max_red")
        s_chain = sem("s_chain")
        s_neg_max = sem("s_neg_max")
        s_max_turned = sem("s_max_turned")
        s_max_copied = sem("s_max_copied")
        s_score = [sem(f"s_score{n}") for n in range(2)]
        s_exp = sem("s_exp")
        s_sums = sem("s_sums")
        s_pv = sem("s_pv")
        s_sums_copied = sem("s_sums_copied")
        s_pv_copied = sem("s_pv_copied")
        s_recip = sem("s_recip")
        s_attn = sem("s_attn")
        s_out_mm = sem("s_out_mm")
        s_z = sem("s_z")
        s_stats = sem("s_stats")
        s_moments = sem("s_moments")
        s_var = sem("s_var")
        s_rstd = sem("s_rstd")
        s_mu_rstd = sem("s_mu_rstd")
        s_shift = sem("s_shift")
        s_zn = sem("s_zn")
        s_zg = sem("s_zg")
        s_y = sem("s_y")
        s_stored = [sem(f"s_stored{n}") for n in range(2)]

        block = ctx.enter_context(nc.Block())

        def slots(eng, slot):
            for i in range(UNROLL):
                slot(Batch(0, i))
            with eng.Fori(0, B // UNROLL - 2) as t:
                for u in range(UNROLL):
                    slot(Batch(t, UNROLL + u))
            for i in range(B - UNROLL, B):
                slot(Batch(0, i))

        @block.sync
        def _(sp):
            for w, d in ((wq_sb, wq), (wk_sb, wk), (wv_sb, wv), (wo_sb, wo)):
                sp.dma_start(w[:, :, :], d.rearrange("(t p) n -> p t n", p=P)).then_inc(s_weights, 16)
            sp.dma_start(gamma_sb[:, :], gamma.partition_broadcast(P)).then_inc(s_weights, 16)
            sp.dma_start(beta_sb[:, :], beta.partition_broadcast(P)).then_inc(s_weights, 16)

            x_v = x.rearrange("b (t p) d -> b p t d", p=P)
            c_v = ctx_in.rearrange("b (k p) d -> b p k d", p=BK)
            m_v = mask.rearrange("b (t p) k -> b p t k", p=P)
            o_v = out.rearrange("b (t p) d -> b p t d", p=P)

            def load(b):
                n, at = b.ring, bass.ds(b.n, 1)
                sp.dma_start(x_in[n][:, :, :], x_v[at, :, :, :].squeeze(0)).then_inc(s_loaded[n], 16)
                sp.dma_start(c_in[n][:, :, :], c_v[at, :, :, :].squeeze(0)).then_inc(s_loaded[n], 16)
                sp.dma_start(m_in[n][:, :, :], m_v[at, :, :, :].squeeze(0)).then_inc(s_loaded[n], 16)

            def store(b):
                sp.wait_ge(s_y, b.n + 1)
                sp.dma_start(o_v[bass.ds(b.n, 1), :, :, :].squeeze(0),
                             y[b.side][:, :, :]).then_inc(s_stored[b.side], 16)

            def slot(i):
                if i.from_(UNROLL):
                    sp.wait_ge(s_z, i.n - (UNROLL - 1))
                load(i)
                if i.from_(UNROLL):
                    store(i - UNROLL)

            slots(sp, slot)
            for b in range(B - UNROLL, B):
                store(Batch(0, b))
            for n in range(2):
                sp.wait_ge(s_stored[n], 16 * (B // 2))

        @block.gpsimd
        def _(pool):
            made = [0]

            def step(ins):
                made[0] += 1
                ins.then_inc(s_const, 1)
                pool.wait_ge(s_const, made[0])

            step(pool.memset(ident[:, :], 0.0))
            step(pool.affine_select(out=ident[:, :], in_=ident[:, :], compare_op=ALU.not_equal, fill=1.0, base=0,
                                    pattern=[[-1, P]], channel_multiplier=1))
            step(pool.memset(head_rows[:, :], 1.0))
            step(pool.affine_select(out=head_rows[:, :], in_=head_rows[:, :], compare_op=ALU.is_ge, fill=0.0, base=0,
                                    pattern=[[-HD, HG]], channel_multiplier=1))
            step(pool.affine_select(out=head_rows[:, :], in_=head_rows[:, :], compare_op=ALU.is_ge, fill=0.0,
                                    base=HD - 1, pattern=[[HD, HG]], channel_multiplier=-1))
            step(pool.memset(spread32[:, :, :], 0.0))
            for half in range(2):
                v = spread32[0:BK, :, half * BK:(half + 1) * BK]
                step(pool.affine_select(out=v, in_=v, compare_op=ALU.not_equal, fill=1.0, base=0,
                                        pattern=[[0, NP], [-1, BK]], channel_multiplier=1))
                v = spread32[BK:NM, :, half * BK:(half + 1) * BK]
                step(pool.affine_select(out=v, in_=v, compare_op=ALU.not_equal, fill=1.0, base=-half,
                                        pattern=[[-2, NP], [0, BK]], channel_multiplier=1))
            step(pool.memset(ones_pair[:, :], 0.0))
            for half in range(2):
                step(pool.memset(ones_pair[half * BK:(half + 1) * BK, half * HD:(half + 1) * HD], 1.0))
            step(pool.memset(half_neg[:, :], -0.5))
            step(pool.memset(neg_one[:, :], -1.0))
            for n in range(2):
                step(pool.memset(v_pair[n][:, :, :, :], 0.0))
            pool.wait_ge(s_weights, 96)

            def spread_k(b):
                pool.wait_ge(s_k_copied, b.n + 1)
                for kb in range(KB):
                    for g in range(NG):
                        last = pool.tensor_tensor(
                            k32[b.side][:, kb, g, :, :],
                            kT[:, g, kb, :].unsqueeze(1).to_broadcast([P, HG, BK]),
                            head_rows[:, :].unsqueeze(2).to_broadcast([P, HG, BK]), ALU.mult)
                last.then_inc(s_k_spread, 1)

            def scales(b):
                m = b.side
                pool.wait_ge(s_var, b.n + 1)
                if b.from_(2):
                    pool.wait_ge(s_zn, b.n - 1)
                pool.tensor_tensor(rstd[m][:, :], var_eps[m][:, :], half_neg[:, :], ALU.pow).then_inc(s_rstd, 1)
                pool.wait_ge(s_rstd, b.n + 1)
                pool.tensor_tensor(mu_rstd[m][:, :], moments[m][:, :, 0], rstd[m][:, :],
                                   ALU.mult).then_inc(s_mu_rstd, 1)
                pool.wait_ge(s_mu_rstd, b.n + 1)
                pool.tensor_tensor(shift[m][:, :], mu_rstd[m][:, :], neg_one[:, :], ALU.mult).then_inc(s_shift, 1)

            def affine(b):
                m = b.side
                pool.wait_ge(s_zn, b.n + 1)
                pool.tensor_tensor(zg[:, :, :], zn[m][:, :, :], gamma_sb[:, :].unsqueeze(1).to_broadcast([P, QT, D]),
                                   ALU.mult).then_inc(s_zg, 1)
                pool.wait_ge(s_zg, b.n + 1)
                if b.from_(2):
                    pool.wait_ge(s_stored[m], b.turn * 16)
                pool.tensor_tensor(y[m][:, :, :], zg[:, :, :], beta_sb[:, :].unsqueeze(1).to_broadcast([P, QT, D]),
                                   ALU.add).then_inc(s_y, 1)

            spread_k(Batch(0, 0))

            def slot(i):
                more = (i + 1).exists(B)
                if i.from_(2):
                    scales(i - 2)
                if more:
                    spread_k(i + 1)
                if i.from_(2):
                    affine(i - 2)

            slots(pool, slot)
            for b in range(B - 2, B):
                scales(Batch(0, b))
                affine(Batch(0, b))

        @block.scalar
        def _(act):
            def mask_addend(b):
                act.wait_ge(s_loaded[b.ring], (b.round + 1) * 48)
                act.activation(mask_b[b.side][:, :, :], m_in[b.ring][:, :, :], ACT.Copy, scale=-BIG).then_inc(s_mask, 1)

            def copies(b):
                act.wait_ge(s_x_turned, b.n + 1)
                act.activation(xT[:, :, :], p_x[:, :].rearrange("p (t s) -> p t s", t=DT),
                               ACT.Copy).then_inc(s_x_copied, 1)
                act.wait_ge(s_c_turned, b.n + 1)
                for t in range(DT):
                    last = act.activation(
                        cT[:, t, :, :, :],
                        p_k[:, t * SK:(t + 1) * SK].rearrange("p (k c) -> p k c", k=KB).unsqueeze(2)
                        .to_broadcast([P, KB, 2, BK]), ACT.Copy)
                last.then_inc(s_c_copied, 1)
                act.wait_ge(s_m_turned, b.n + 1)
                act.activation(addend[b.side][0:BK, :, :], mask_ps[0:BK, 0:KB * S].rearrange("p (k s) -> p k s", k=KB),
                               ACT.Copy).then_inc(s_m_copied, 1)

            def exps(b, kb):
                half = NP // 2
                for a in range(2):
                    act.wait_ge(s_score[a], b.n * KB + (kb + 1))
                    last = act.activation(
                        probs[:, a * half:(a + 1) * half, :],
                        sc[:, a * half * S:(a + 1) * half * S].rearrange("p (j s) -> p j s", j=half),
                        ACT.Exp, scale=SCALE)
                last.then_inc(s_exp, 1)

            def attn_copies(b):
                act.wait_ge(s_sums, b.n + 1)
                if b.from_(1):
                    act.wait_ge(s_attn, b.n)
                act.activation(sums[:, :], p_x[:, :], ACT.Copy).then_inc(s_sums_copied, 1)
                act.wait_ge(s_pv, (b.n + 1) * KB)
                act.activation(attn_raw[:, :], p_k[:, :], ACT.Copy).then_inc(s_pv_copied, 1)

            def normalise(b):
                m = b.side
                act.wait_ge(s_shift, b.n + 1)
                if b.from_(2):
                    act.wait_ge(s_zg, b.n - 1)
                for t in range(QT):
                    last = act.activation(zn[m][:, t, :], z[m][:, t, :], ACT.Identity, bias=shift[m][:, t:t + 1],
                                          scale=rstd[m][:, t:t + 1])
                last.then_inc(s_zn, 1)

            mask_addend(Batch(0, 0))
            mask_addend(Batch(0, 1))
            copies(Batch(0, 0))

            def slot(i):
                if (i + 1).exists(B):
                    copies(i + 1)
                exps(i, 0)
                if (i + 2).exists(B):
                    mask_addend(i + 2)
                if i.from_(2):
                    normalise(i - 2)
                for kb in range(1, KB):
                    exps(i, kb)
                attn_copies(i)

            slots(act, slot)
            for b in range(B - 2, B):
                normalise(Batch(0, b))

        @block.vector
        def _(dve):
            dve.wait_ge(s_const, N_CONST)
            dve.tensor_copy(ident_b[:, :], ident[:, :]).then_inc(s_const_r, 1)
            dve.tensor_copy(spread[:, :, :], spread32[:, :, :]).then_inc(s_const_r, 1)

            def projections(b):
                m = b.side
                dve.wait_ge(s_k_proj, b.n + 1)
                if b.from_(1):
                    dve.wait_ge(s_k_spread, b.n)
                dve.tensor_copy(kT[:, :, :, :], p_k[:, 0:NG * SK].rearrange("p (g k c) -> p g k c", g=NG, k=KB)
                                ).then_inc(s_k_copied, 1)
                dve.wait_ge(s_q_proj, b.n + 1)
                dve.tensor_copy(q32[m][:, :, :], p_q[:, :].rearrange("p (g s) -> p g s", g=NG)).then_inc(s_q_copied, 1)
                dve.wait_ge(s_q_copied, b.n + 1)
                dve.tensor_copy(q16[:, :, :], q32[m][:, :, :]).then_inc(s_q_cast, 1)
                for kb in range(KB):
                    dve.wait_ge(s_v_proj, b.n * KB + (kb + 1))
                    for half in range(2):
                        r = slice(half * BK, (half + 1) * BK)
                        last = dve.tensor_copy(
                            v_pair[m][r, kb, :, half * HD:(half + 1) * HD],
                            p_y[r, 0:D].rearrange("p (j h d) -> p j h d", h=2, d=HD)[:, :, half, :])
                    last.then_inc(s_v_copied, 1)
                dve.wait_ge(s_k_spread, b.n + 1)
                dve.tensor_copy(k16[:, :, :, :, :].rearrange("p k g h c -> p (k g h c)"),
                                k32[m][:, :, :, :, :].rearrange("p k g h c -> p (k g h c)")).then_inc(s_k_cast, 1)

            def maxima(b):
                for kb in range(KB):
                    dve.wait_ge(s_max_mm, b.n * KB + (kb + 1))
                    dve.tensor_reduce(row_max[:, kb, :], sc[:, :].rearrange("p (r c) -> p r c", c=BK), AX.X,
                                      ALU.max).then_inc(s_max_red, 1)
                dve.wait_ge(s_max_red, (b.n + 1) * KB)
                dve.tensor_reduce(all_max[:, :], row_max[:, :, :].rearrange("p k r -> p r k"), AX.X,
                                  ALU.max).then_inc(s_chain, 1)
                dve.wait_ge(s_chain, b.n + 1)
                dve.tensor_scalar(neg_max[:, :], all_max[:, :], -BIG / 2, -1.0, ALU.max,
                                  ALU.mult).then_inc(s_neg_max, 1)

            def max_rows(b):
                dve.wait_ge(s_max_turned, b.n + 1)
                dve.tensor_copy(addend[b.side][BK:NM, :, :], p_q[0:H, 0:S].unsqueeze(1).to_broadcast([H, KB, S])
                                ).then_inc(s_max_copied, 1)

            def residual(b):
                m = b.side
                dve.wait_ge(s_out_mm, b.n + 1)
                if b.from_(2):
                    dve.wait_ge(s_zn, b.n - 1)
                dve.tensor_tensor(z[m][:, :, :], p_y[:, :].rearrange("p (t d) -> p t d", t=QT),
                                  x_in[b.ring][:, :, :], ALU.add).then_inc(s_z, 1)

            def quotients(b):
                dve.wait_ge(s_sums_copied, b.n + 1)
                dve.reciprocal(recips[:, :], sums[:, :]).then_inc(s_recip, 1)
                dve.wait_ge(s_recip, b.n + 1)
                dve.wait_ge(s_pv_copied, b.n + 1)
                if b.from_(1):
                    dve.wait_ge(s_out_mm, b.n)
                dve.tensor_tensor(attn[:, :], attn_raw[:, :], recips[:, :], ALU.mult).then_inc(s_attn, 1)

            def statistics(b):
                dve.wait_ge(s_z, b.n + 1)
                for t in range(QT):
                    last = dve.bn_stats(stats[:, t, :], z[b.side][:, t, :])
                last.then_inc(s_stats, 1)

            def moments_waits(b):
                dve.wait_ge(s_stats, b.n + 1)
                if b.from_(2):
                    dve.wait_ge(s_shift, b.n - 1)

            def variance(b):
                m = b.side
                for t in range(QT):
                    last = dve.bn_aggr(moments[m][:, t, :], stats[:, t, :])
                last.then_inc(s_moments, 1)
                dve.wait_ge(s_moments, b.n + 1)
                dve.tensor_scalar(var_eps[m][:, :], moments[m][:, :, 1], EPS, None, ALU.add).then_inc(s_var, 1)

            projections(Batch(0, 0))
            maxima(Batch(0, 0))

            def slot(i):
                if i.from_(2):
                    residual(i - 2)
                    statistics(i - 2)
                    moments_waits(i - 2)
                max_rows(i)
                if i.from_(2):
                    variance(i - 2)
                if i.from_(1):
                    quotients(i - 1)
                if (i + 1).exists(B):
                    projections(i + 1)
                    maxima(i + 1)

            slots(dve, slot)
            for b in (Batch(0, B - 2), Batch(0, B - 1)):
                if b.c == B - 1:
                    quotients(b)
                residual(b)
                statistics(b)
                moments_waits(b)
                variance(b)

        @block.tensor
        def _(pe):
            pe.wait_ge(s_const, N_CONST)
            pe.wait_ge(s_const_r, 2)
            pe.wait_ge(s_weights, 96)

            def turn(b):
                n = b.ring
                pe.wait_ge(s_loaded[n], (b.round + 1) * 48)
                pe.wait_ge(s_mask, b.n + 1)
                if b.from_(2):
                    pe.wait_ge(s_sums_copied, b.n - 1)
                    pe.wait_ge(s_pv_copied, b.n - 1)
                if b.from_(1):
                    pe.wait_ge(s_v_copied, b.n * KB)
                for t in range(DT):
                    for q in range(QT):
                        last = pe.transpose(p_x[:, t * S + q * P:t * S + (q + 1) * P],
                                            x_in[n][:, q, t * P:(t + 1) * P], ident[:, :])
                last.then_inc(s_x_turned, 1)
                for t in range(DT):
                    for kb in range(KB):
                        last = pe.transpose(p_k[:, t * SK + kb * BK:t * SK + (kb + 1) * BK],
                                            c_in[n][:, kb, t * P:(t + 1) * P], ident[0:BK, 0:BK])
                last.then_inc(s_c_turned, 1)
                for kb in range(KB):
                    for q in range(QT):
                        last = pe.transpose(mask_ps[0:BK, kb * S + q * P:kb * S + (q + 1) * P],
                                            mask_b[b.side][:, q, kb * BK:(kb + 1) * BK], ident_b[:, :])
                last.then_inc(s_m_turned, 1)

            def project(b):
                pe.wait_ge(s_c_copied, b.n + 1)
                for g in range(NG):
                    for t in range(DT):
                        last = pe.matmul(p_k[:, g * SK:(g + 1) * SK], wk_sb[:, t, g * P:(g + 1) * P],
                                         cT[:, t, :, 0, :], start=(t == 0), stop=(t == DT - 1))
                last.then_inc(s_k_proj, 1)
                pe.wait_ge(s_x_copied, b.n + 1)
                if b.from_(1):
                    pe.wait_ge(s_max_copied, b.n)
                for g in range(NG):
                    for t in range(DT):
                        last = pe.matmul(p_q[:, g * S:(g + 1) * S], wq_sb[:, t, g * P:(g + 1) * P], xT[:, t, :],
                                         start=(t == 0), stop=(t == DT - 1))
                last.then_inc(s_q_proj, 1)
                pe.wait_ge(s_m_copied, b.n + 1)
                for kb in range(KB):
                    if kb:
                        pe.wait_ge(s_v_copied, b.n * KB + kb)
                    for t in range(DT):
                        last = pe.matmul(p_y[:, 0:D], cT[:, t, kb, :, :], wv_sb[:, t, :], start=(t == 0),
                                         stop=(t == DT - 1))
                    last.then_inc(s_v_proj, 1)

            def max_scores(b):
                pe.wait_ge(s_q_cast, b.n + 1)
                pe.wait_ge(s_k_cast, b.n + 1)
                for kb in range(KB):
                    if kb:
                        pe.wait_ge(s_max_red, b.n * KB + kb)
                    for q in range(QT):
                        for g in range(NG):
                            a = (q * NG + g) * HG * BK
                            pe.matmul(sc[:, a:a + HG * BK], ident_b[:, :],
                                      mask_b[b.side][:, q, kb * BK:(kb + 1) * BK].unsqueeze(1)
                                      .to_broadcast([P, HG, BK]), start=True, stop=False)
                            last = pe.matmul(sc[:, a:a + HG * BK], q16[:, g, q * P:(q + 1) * P], k16[:, kb, g, :, :],
                                             start=False, stop=True)
                    last.then_inc(s_max_mm, 1)

            def turn_max(b):
                pe.wait_ge(s_neg_max, b.n + 1)
                for q in range(QT):
                    last = pe.transpose(p_q[0:H, q * P:(q + 1) * P], neg_max[:, q * H:(q + 1) * H], ident[:, :])
                last.then_inc(s_max_turned, 1)

            def scores(b, kb):
                m = b.side
                if kb == 0:
                    pe.wait_ge(s_max_copied, b.n + 1)
                    pe.wait_ge(s_m_copied, b.n + 1)
                else:
                    pe.wait_ge(s_exp, b.n * KB + kb)
                for j in range(NP):
                    o = sc[:, j * S:(j + 1) * S]
                    g, c = j // (NP // NG), j % (NP // NG)
                    pe.matmul(o, spread[:, j, :], addend[m][:, kb, :], start=True, stop=False)
                    last = pe.matmul(o, k32[m][:, kb, g, 2 * c:2 * c + 2, :], q32[m][:, g, :], start=False, stop=True)
                    if j % (NP // 2) == NP // 2 - 1:
                        last.then_inc(s_score[j // (NP // 2)], 1)

            def weigh(b, kb, last_batch):
                pe.wait_ge(s_exp, b.n * KB + (kb + 1))
                if kb == 0 and not last_batch:
                    pe.wait_ge(s_x_copied, b.n + 2)
                    pe.wait_ge(s_k_copied, b.n + 2)
                for j in range(NP):
                    g, c = j // (NP // NG), j % (NP // NG)
                    last = pe.matmul(p_x[c * PQ:(c + 1) * PQ, g * S:(g + 1) * S], ones_pair[:, :], probs[:, j, :],
                                     start=(kb == 0 and g == 0), stop=(kb == KB - 1), skip_group_check=True)
                if kb == KB - 1:
                    last.then_inc(s_sums, 1)
                for j in range(NP):
                    g, c = j // (NP // NG), j % (NP // NG)
                    last = pe.matmul(p_k[c * PQ:(c + 1) * PQ, g * S:(g + 1) * S], v_pair[b.side][:, kb, j, :],
                                     probs[:, j, :], start=(kb == 0 and g == 0), stop=(kb == KB - 1),
                                     skip_group_check=True)
                last.then_inc(s_pv, 1)

            def out_project(b):
                pe.wait_ge(s_attn, b.n + 1)
                for q in range(QT):
                    for g in range(NG):
                        last = pe.matmul(p_y[:, q * D:(q + 1) * D], attn[:, g * S + q * P:g * S + (q + 1) * P],
                                         wo_sb[:, g, :], start=(g == 0), stop=(g == NG - 1))
                last.then_inc(s_out_mm, 1)

            turn(Batch(0, 0))
            project(Batch(0, 0))
            max_scores(Batch(0, 0))

            def slot(i):
                more = (i + 1).exists(B)
                if more:
                    turn(i + 1)
                if i.from_(2):
                    if more:
                        pe.wait_ge(s_m_copied, i.n + 2)
                    out_project(i - 2)
                turn_max(i)
                scores(i, 0)
                if more:
                    if i.from_(2):
                        pe.wait_ge(s_z, i.n - 1)
                    project(i + 1)
                weigh(i, 0, not more)
                for kb in range(1, KB):
                    scores(i, kb)
                    weigh(i, kb, not more)
                if more:
                    max_scores(i + 1)

            slots(pe, slot)
            out_project(Batch(0, B - 2))
            pe.wait_ge(s_z, B - 1)
            out_project(Batch(0, B - 1))


_INS = ['x', 'ctx_1024', 'mask_BxSxS2_bk1', 'L0_xattn_wq', 'L0_xattn_wk', 'L0_xattn_wv', 'L0_xattn_wo',
        'L0_xattn_gamma', 'L0_xattn_beta']


def kernel(**inputs):
    import numpy as np
    import concourse.bacc as bacc
    from concourse.bass_utils import run_bass_kernel_spmd

    nc = bacc.Bacc("TRN2", target_bir_lowering=False, num_devices=1)
    arrays, args = {}, []
    for name in _INS:
        a = np.ascontiguousarray(inputs[name])
        arrays[name] = a
        args.append(nc.dram_tensor(name, a.shape, mybir.dt.from_np(a.dtype), kind="ExternalInput").ap())
    shape = inputs['x'].shape
    out = nc.dram_tensor("out", shape, F32, kind="ExternalOutput").ap()
    build(nc, *args, out)
    r = run_bass_kernel_spmd(nc, [arrays], core_ids=[0])
    return r.results[0]["out"]
```

```python
import concourse.bass as bass
from concourse import mybir
from contextlib import ExitStack

F32 = mybir.dt.float32
F32R = mybir.dt.float32r
BF16 = mybir.dt.bfloat16
U8 = mybir.dt.uint8
U16 = mybir.dt.uint16
I32 = mybir.dt.int32
ACT = mybir.ActivationFunctionType
ALU = mybir.AluOpType
AX = mybir.AxisListType

P = 128
BIG = 2.0 ** 100
EPS = 1e-5
N_CONST = 17
UNROLL = 4


class Batch:

    def __init__(self, t, c):
        self.t, self.c = t, c
        self.n = c if isinstance(t, int) and t == 0 else t * UNROLL + c
        self.ring = c % UNROLL
        self.side = c % 2
        self.round = c // UNROLL if isinstance(t, int) else t + c // UNROLL
        self.turn = c // 2 if isinstance(t, int) else t * (UNROLL // 2) + c // 2

    def __add__(self, n):
        return Batch(self.t, self.c + n)

    def __sub__(self, n):
        return Batch(self.t, self.c - n)

    def from_(self, n):
        return self.c >= n

    def exists(self, batches):
        return not isinstance(self.t, int) or self.c < batches


def build(nc, x, ctx_in, mask, wq, wk, wv, wo, gamma, beta, out):
    B, S, D = x.shape
    SK = ctx_in.shape[1]
    H, HD = 16, 16
    SCALE = float(HD) ** -0.5
    QT = S // P
    DT = D // P
    BK = 64
    ALL = SK // BK
    HG = P // HD
    NG = H // HG
    NP = H // 2
    PQ = 32
    LOOKS = 4
    NM = BK + H

    ctx = ExitStack()
    with ctx:
        def sb(name, shape, dt=F32):
            return ctx.enter_context(nc.sbuf_tensor(name, shape, dt))

        def pb(name, shape, dt=F32):
            return ctx.enter_context(nc.psum_tensor(name, shape, dt))

        def sem(name):
            return ctx.enter_context(nc.semaphore(name))

        ident = sb("ident", [P, P])
        ident_b = sb("ident_b", [P, P], BF16)
        head_rows = sb("head_rows", [P, HG])
        spread32 = sb("spread32", [NM, NP, P])
        spread = sb("spread", [NM, NP, P], F32R)
        ones_pair = sb("ones_pair", [P, PQ])
        half_neg = sb("half_neg", [P, QT])
        neg_one = sb("neg_one", [P, QT])
        wq_in = sb("wq_in", [P, DT, D])
        wk_in = sb("wk_in", [P, DT, D])
        wv_sb = sb("wv_sb", [P, DT, D])
        wo_sb = sb("wo_sb", [P, DT, D])
        gamma_sb = sb("gamma_sb", [P, D])
        beta_sb = sb("beta_sb", [P, D])
        x_in = [sb(f"x_in{n}", [P, QT, D]) for n in range(UNROLL)]
        c_in = [sb(f"c_in{n}", [BK, ALL, D]) for n in range(UNROLL)]
        m_in = sb("m_in", [P, B * QT, SK], U8)
        mask_b = [sb(f"mask_b{n}", [P, QT, SK], BF16) for n in range(2)]
        xT = sb("xT", [P, DT, S])
        cT = sb("cT", [P, DT, ALL, 2, BK])
        q_hi = [sb(f"q_hi{n}", [P, NG, S], F32R) for n in range(2)]
        q_lo = [sb(f"q_lo{n}", [P, NG, S], F32R) for n in range(2)]
        kT_hi = sb("kT_hi", [P, NG, ALL, BK], F32R)
        kT_lo = sb("kT_lo", [P, NG, ALL, BK], F32R)
        k_hi = [sb(f"k_hi{n}", [P, ALL, NG, HG, BK], F32R) for n in range(2)]
        k_lo = [sb(f"k_lo{n}", [P, ALL, NG, HG, BK], F32R) for n in range(2)]
        v_pair = [sb(f"v_pair{n}", [P, ALL, NP, PQ]) for n in range(2)]
        addend = [sb(f"addend{n}", [NM, ALL, S], F32R) for n in range(2)]
        row_max = sb("row_max", [P, ALL, QT * H])
        all_max = sb("all_max", [P, QT * H])
        neg_max = sb("neg_max", [P, QT * H])
        probs = sb("probs", [P, NP, S])
        sums = sb("sums", [P, NG * S])
        recips = sb("recips", [P, NG * S])
        attn_raw = sb("attn_raw", [P, NG * S])
        attn = sb("attn", [P, NG * S])
        z = [sb(f"z{n}", [P, QT, D]) for n in range(2)]
        stats = sb("stats", [P, QT, 6])
        moments = [sb(f"moments{n}", [P, QT, 2]) for n in range(2)]
        var_eps = [sb(f"var_eps{n}", [P, QT]) for n in range(2)]
        rstd = [sb(f"rstd{n}", [P, QT]) for n in range(2)]
        mu_rstd = [sb(f"mu_rstd{n}", [P, QT]) for n in range(2)]
        shift = [sb(f"shift{n}", [P, QT]) for n in range(2)]
        zn = [sb(f"zn{n}", [P, QT, D]) for n in range(2)]
        zg = sb("zg", [P, QT, D])
        y = [sb(f"y{n}", [P, QT, D]) for n in range(2)]
        least = sb("least", [P, LOOKS])
        least_row = sb("least_row", [P, 1])
        least_all = sb("least_all", [1, 1])
        one_block = sb("one_block", [1, 1], I32)
        sc = pb("sc", [P, NP * S])
        p_x = pb("p_x", [P, 512])
        p_q = pb("p_q", [P, 512])
        p_y = pb("p_y", [P, 512])
        p_k = pb("p_k", [P, 512])
        mask_ps = p_y[:, :].bitcast(BF16)

        s_const = sem("s_const")
        s_const_r = sem("s_const_r")
        s_weights = sem("s_weights")
        s_affine = sem("s_affine")
        s_mask_in = [sem(f"s_mask_in{n}") for n in range(LOOKS)]
        s_look = sem("s_look")
        s_look_turned = sem("s_look_turned")
        s_one_block = sem("s_one_block")
        s_x_loaded = [sem(f"s_x_loaded{n}") for n in range(UNROLL)]

        class Way:

            def __init__(self, name, blocks):
                def sem_(what):
                    return sem(f"{name}_{what}")

                self.KB = blocks
                self.K0 = SK - blocks * BK
                self.c_loaded = [sem_(f"c_loaded{n}") for n in range(UNROLL)]
                self.mask = sem_("mask")
                self.x_turned = sem_("x_turned")
                self.c_turned = sem_("c_turned")
                self.m_turned = sem_("m_turned")
                self.x_copied = sem_("x_copied")
                self.c_copied = sem_("c_copied")
                self.m_copied = sem_("m_copied")
                self.k_proj = sem_("k_proj")
                self.q_proj = sem_("q_proj")
                self.v_proj = sem_("v_proj")
                self.k_rounded = sem_("k_rounded")
                self.k_copied = sem_("k_copied")
                self.k_hi_spread = sem_("k_hi_spread")
                self.k_lo_spread = sem_("k_lo_spread")
                self.q_rounded = sem_("q_rounded")
                self.q_copied = sem_("q_copied")
                self.v_copied = sem_("v_copied")
                self.max_mm = sem_("max_mm")
                self.max_red = sem_("max_red")
                self.all_max = sem_("all_max")
                self.neg_max = sem_("neg_max")
                self.max_turned = sem_("max_turned")
                self.max_copied = sem_("max_copied")
                self.score = [sem_(f"score{n}") for n in range(2)]
                self.exp = sem_("exp")
                self.sums = sem_("sums")
                self.pv = sem_("pv")
                self.sums_copied = sem_("sums_copied")
                self.pv_copied = sem_("pv_copied")
                self.recip = sem_("recip")
                self.attn = sem_("attn")
                self.out_mm = sem_("out_mm")
                self.z = sem_("z")
                self.stats = sem_("stats")
                self.moments = sem_("moments")
                self.var = sem_("var")
                self.rstd = sem_("rstd")
                self.mu_rstd = sem_("mu_rstd")
                self.shift = sem_("shift")
                self.zn = sem_("zn")
                self.zg = sem_("zg")
                self.y = sem_("y")
                self.stored = [sem_(f"stored{n}") for n in range(2)]

        last_block, all_blocks = Way("last", 1), Way("all", ALL)

        block = ctx.enter_context(nc.Block())

        def slots(eng, slot):
            for i in range(UNROLL):
                slot(Batch(0, i))
            with eng.Fori(0, B // UNROLL - 2) as t:
                for u in range(UNROLL):
                    slot(Batch(t, UNROLL + u))
            for i in range(B - UNROLL, B):
                slot(Batch(0, i))

        def take_way(eng, program):
            eng.wait_ge(s_one_block, 1)
            found = eng.value_load(one_block[0:1, 0:1], min_val=0, max_val=1)
            with eng.If(found != 0):
                program(last_block)
            with eng.Else():
                program(all_blocks)

        @block.sync
        def _(sp):
            x_v = x.rearrange("b (t p) d -> b p t d", p=P)
            c_v = ctx_in.rearrange("b (k p) d -> b p k d", p=BK)
            o_v = out.rearrange("b (t p) d -> b p t d", p=P)

            def load_x(b):
                sp.dma_start(x_in[b.ring][:, :, :],
                             x_v[bass.ds(b.n, 1), :, :, :].squeeze(0)).then_inc(s_x_loaded[b.ring], 16)

            for to, d in ((wq_in, wq), (wk_in, wk), (wv_sb, wv), (wo_sb, wo)):
                sp.dma_start(to[:, :, :], d.rearrange("(t p) n -> p t n", p=P)).then_inc(s_weights, 16)
            for i in range(UNROLL):
                load_x(Batch(0, i))

            def program(w):
                def load_ctx(b):
                    sp.dma_start(c_in[b.ring][:, ALL - w.KB:, :],
                                 c_v[bass.ds(b.n, 1), :, ALL - w.KB:, :].squeeze(0)).then_inc(w.c_loaded[b.ring], 16)

                def store(b):
                    sp.wait_ge(w.y, b.n + 1)
                    sp.dma_start(o_v[bass.ds(b.n, 1), :, :, :].squeeze(0),
                                 y[b.side][:, :, :]).then_inc(w.stored[b.side], 16)

                def slot(i):
                    if i.from_(UNROLL):
                        sp.wait_ge(w.z, i.n - (UNROLL - 1))
                        load_x(i)
                    load_ctx(i)
                    if i.from_(UNROLL):
                        store(i - UNROLL)

                slots(sp, slot)
                for b in range(B - UNROLL, B):
                    store(Batch(0, b))
                for n in range(2):
                    sp.wait_ge(w.stored[n], 16 * (B // 2))

            take_way(sp, program)

        @block.gpsimd
        def _(pool):
            made = [0]

            def step(ins):
                made[0] += 1
                ins.then_inc(s_const, 1)
                pool.wait_ge(s_const, made[0])

            step(pool.memset(ident[:, :], 0.0))
            step(pool.affine_select(out=ident[:, :], in_=ident[:, :], compare_op=ALU.not_equal, fill=1.0, base=0,
                                    pattern=[[-1, P]], channel_multiplier=1))
            step(pool.memset(head_rows[:, :], 1.0))
            step(pool.affine_select(out=head_rows[:, :], in_=head_rows[:, :], compare_op=ALU.is_ge, fill=0.0, base=0,
                                    pattern=[[-HD, HG]], channel_multiplier=1))
            step(pool.affine_select(out=head_rows[:, :], in_=head_rows[:, :], compare_op=ALU.is_ge, fill=0.0,
                                    base=HD - 1, pattern=[[HD, HG]], channel_multiplier=-1))
            step(pool.memset(spread32[:, :, :], 0.0))
            for half in range(2):
                v = spread32[0:BK, :, half * BK:(half + 1) * BK]
                step(pool.affine_select(out=v, in_=v, compare_op=ALU.not_equal, fill=1.0, base=0,
                                        pattern=[[0, NP], [-1, BK]], channel_multiplier=1))
                v = spread32[BK:NM, :, half * BK:(half + 1) * BK]
                step(pool.affine_select(out=v, in_=v, compare_op=ALU.not_equal, fill=1.0, base=-half,
                                        pattern=[[-2, NP], [0, BK]], channel_multiplier=1))
            step(pool.memset(ones_pair[:, :], 0.0))
            for half in range(2):
                step(pool.memset(ones_pair[half * BK:(half + 1) * BK, half * HD:(half + 1) * HD], 1.0))
            step(pool.memset(half_neg[:, :], -0.5))
            step(pool.memset(neg_one[:, :], -1.0))
            for n in range(2):
                step(pool.memset(v_pair[n][:, :, :, :], 0.0))
            pool.wait_ge(s_affine, 32)

            def program(w):
                KB = w.KB

                def spread_k(b):
                    for kT, to, copied, spread_ in ((kT_hi, k_hi, w.k_rounded, w.k_hi_spread),
                                                    (kT_lo, k_lo, w.k_copied, w.k_lo_spread)):
                        pool.wait_ge(copied, b.n + 1)
                        for kb in range(KB):
                            for g in range(NG):
                                last = pool.tensor_tensor(
                                    to[b.side][:, kb, g, :, :],
                                    kT[:, g, kb, :].bitcast(F32).unsqueeze(1).to_broadcast([P, HG, BK]),
                                    head_rows[:, :].unsqueeze(2).to_broadcast([P, HG, BK]), ALU.mult)
                        last.then_inc(spread_, 1)

                def scales(b):
                    m = b.side
                    pool.wait_ge(w.var, b.n + 1)
                    if b.from_(2):
                        pool.wait_ge(w.zn, b.n - 1)
                    pool.tensor_tensor(rstd[m][:, :], var_eps[m][:, :], half_neg[:, :], ALU.pow).then_inc(w.rstd, 1)
                    pool.wait_ge(w.rstd, b.n + 1)
                    pool.tensor_tensor(mu_rstd[m][:, :], moments[m][:, :, 0], rstd[m][:, :],
                                       ALU.mult).then_inc(w.mu_rstd, 1)
                    pool.wait_ge(w.mu_rstd, b.n + 1)
                    pool.tensor_tensor(shift[m][:, :], mu_rstd[m][:, :], neg_one[:, :], ALU.mult).then_inc(w.shift, 1)

                def affine(b):
                    m = b.side
                    pool.wait_ge(w.zn, b.n + 1)
                    pool.tensor_tensor(zg[:, :, :], zn[m][:, :, :],
                                       gamma_sb[:, :].unsqueeze(1).to_broadcast([P, QT, D]),
                                       ALU.mult).then_inc(w.zg, 1)
                    pool.wait_ge(w.zg, b.n + 1)
                    if b.from_(2):
                        pool.wait_ge(w.stored[m], b.turn * 16)
                    pool.tensor_tensor(y[m][:, :, :], zg[:, :, :],
                                       beta_sb[:, :].unsqueeze(1).to_broadcast([P, QT, D]),
                                       ALU.add).then_inc(w.y, 1)

                spread_k(Batch(0, 0))

                def slot(i):
                    if (i + 1).exists(B):
                        spread_k(i + 1)
                    if i.from_(2):
                        scales(i - 2)
                        affine(i - 2)

                slots(pool, slot)
                for b in range(B - 2, B):
                    scales(Batch(0, b))
                    affine(Batch(0, b))

            take_way(pool, program)

        @block.scalar
        def _(act):
            m_v = mask.rearrange("b (t p) k -> p (b t) k", p=P)
            for n in range(LOOKS):
                r = slice(n * B * QT // LOOKS, (n + 1) * B * QT // LOOKS)
                act.dma_start(m_in[:, r, :], m_v[:, r, :]).then_inc(s_mask_in[n], 16)
            act.dma_start(gamma_sb[:, :], gamma.partition_broadcast(P)).then_inc(s_affine, 16)
            act.dma_start(beta_sb[:, :], beta.partition_broadcast(P)).then_inc(s_affine, 16)
            for n in range(LOOKS):
                act.wait_ge(s_mask_in[n], 16)

            def program(w):
                KB, K0, KS = w.KB, w.K0, w.KB * BK

                def mask_addend(b):
                    act.activation(mask_b[b.side][:, :, 0:KS], m_in[:, bass.ds(b.n * QT, QT), K0:], ACT.Copy,
                                   scale=-BIG).then_inc(w.mask, 1)

                def copies(b):
                    act.wait_ge(w.m_turned, b.n + 1)
                    act.activation(addend[b.side][0:BK, 0:KB, :],
                                   mask_ps[0:BK, 0:KB * S].rearrange("p (k s) -> p k s", k=KB),
                                   ACT.Copy).then_inc(w.m_copied, 1)
                    act.wait_ge(w.c_turned, b.n + 1)
                    for t in range(DT):
                        last = act.activation(
                            cT[:, t, 0:KB, :, :],
                            p_k[:, t * KS:(t + 1) * KS].rearrange("p (k c) -> p k c", k=KB).unsqueeze(2)
                            .to_broadcast([P, KB, 2, BK]), ACT.Copy)
                    last.then_inc(w.c_copied, 1)
                    act.wait_ge(w.x_turned, b.n + 1)
                    act.activation(xT[:, :, :], p_x[:, :].rearrange("p (t s) -> p t s", t=DT),
                                   ACT.Copy).then_inc(w.x_copied, 1)

                def exps(b, kb):
                    half = NP // 2
                    for a in range(2):
                        act.wait_ge(w.score[a], b.n * KB + (kb + 1))
                        last = act.activation(
                            probs[:, a * half:(a + 1) * half, :],
                            sc[:, a * half * S:(a + 1) * half * S].rearrange("p (j s) -> p j s", j=half),
                            ACT.Exp, scale=SCALE)
                    last.then_inc(w.exp, 1)

                def attn_copies(b):
                    act.wait_ge(w.sums, b.n + 1)
                    if b.from_(1):
                        act.wait_ge(w.attn, b.n)
                    act.activation(sums[:, :], p_x[:, :], ACT.Copy).then_inc(w.sums_copied, 1)
                    act.wait_ge(w.pv, (b.n + 1) * KB)
                    act.activation(attn_raw[:, :], p_k[:, :], ACT.Copy).then_inc(w.pv_copied, 1)

                def normalise(b):
                    m = b.side
                    act.wait_ge(w.shift, b.n + 1)
                    if b.from_(2):
                        act.wait_ge(w.zg, b.n - 1)
                    for t in range(QT):
                        last = act.activation(zn[m][:, t, :], z[m][:, t, :], ACT.Identity, bias=shift[m][:, t:t + 1],
                                              scale=rstd[m][:, t:t + 1])
                    last.then_inc(w.zn, 1)

                mask_addend(Batch(0, 0))
                mask_addend(Batch(0, 1))
                copies(Batch(0, 0))

                def slot(i):
                    if (i + 1).exists(B):
                        copies(i + 1)
                    exps(i, 0)
                    if (i + 2).exists(B):
                        mask_addend(i + 2)
                    if i.from_(2):
                        normalise(i - 2)
                    for kb in range(1, KB):
                        exps(i, kb)
                    attn_copies(i)

                slots(act, slot)
                for b in range(B - 2, B):
                    normalise(Batch(0, b))

            take_way(act, program)

        @block.vector
        def _(dve):
            dve.wait_ge(s_const, N_CONST)
            dve.tensor_copy(ident_b[:, :], ident[:, :])
            dve.tensor_copy(spread[:, :, :], spread32[:, :, :]).then_inc(s_const_r, 1)
            for n in range(LOOKS):
                r = slice(n * B * QT // LOOKS, (n + 1) * B * QT // LOOKS)
                dve.wait_ge(s_mask_in[n], 16)
                dve.tensor_reduce(least[:, n:n + 1], m_in[:, r, 0:SK - BK].bitcast(U16), AX.XY,
                                  ALU.min).then_inc(s_look, 1)
            dve.wait_ge(s_look, LOOKS)
            dve.tensor_reduce(least_row[:, :], least[:, :], AX.X, ALU.min).then_inc(s_look, 1)
            dve.wait_ge(s_look_turned, 1)
            dve.tensor_reduce(least_all[:, :], p_q[0:1, 0:P], AX.X, ALU.min).then_inc(s_look, 1)
            dve.wait_ge(s_look, LOOKS + 2)
            dve.tensor_scalar(one_block[:, :], least_all[:, :], 257.0, None, ALU.is_ge).then_inc(s_one_block, 1)

            def program(w):
                KB, KS = w.KB, w.KB * BK

                def k_copies(b):
                    dve.wait_ge(w.k_proj, b.n + 1)
                    if b.from_(1):
                        dve.wait_ge(w.k_lo_spread, b.n)
                    ps = p_k[:, 0:NG * KS].rearrange("p (g k c) -> p g k c", g=NG, k=KB)
                    hi, lo = kT_hi[:, :, 0:KB, :], kT_lo[:, :, 0:KB, :]
                    dve.tensor_copy(hi, ps).then_inc(w.k_rounded, 1)
                    dve.wait_ge(w.k_rounded, b.n + 1)
                    dve.tensor_tensor(lo, ps, hi.bitcast(F32), ALU.subtract).then_inc(w.k_copied, 1)

                def q_copies(b):
                    m = b.side
                    dve.wait_ge(w.q_proj, b.n + 1)
                    ps = p_q[:, :].rearrange("p (g s) -> p g s", g=NG)
                    dve.tensor_copy(q_hi[m][:, :, :], ps).then_inc(w.q_rounded, 1)
                    dve.wait_ge(w.q_rounded, b.n + 1)
                    dve.tensor_tensor(q_lo[m][:, :, :], ps, q_hi[m][:, :, :].bitcast(F32),
                                      ALU.subtract).then_inc(w.q_copied, 1)

                def v_copies(b):
                    for kb in range(KB):
                        dve.wait_ge(w.v_proj, b.n * KB + (kb + 1))
                        for half in range(2):
                            r = slice(half * BK, (half + 1) * BK)
                            last = dve.tensor_copy(
                                v_pair[b.side][r, kb, :, half * HD:(half + 1) * HD],
                                p_y[r, 0:D].rearrange("p (j h d) -> p j h d", h=2, d=HD)[:, :, half, :])
                        last.then_inc(w.v_copied, 1)

                def maxima(b):
                    for kb in range(KB):
                        dve.wait_ge(w.max_mm, b.n * KB + (kb + 1))
                        dve.tensor_reduce(row_max[:, kb, :], sc[:, :].rearrange("p (r c) -> p r c", c=BK), AX.X,
                                          ALU.max).then_inc(w.max_red, 1)
                    dve.wait_ge(w.max_red, (b.n + 1) * KB)
                    if KB > 1:
                        dve.tensor_reduce(all_max[:, :], row_max[:, :, :].rearrange("p k r -> p r k"), AX.X,
                                          ALU.max).then_inc(w.all_max, 1)
                        dve.wait_ge(w.all_max, b.n + 1)
                    dve.tensor_scalar(neg_max[:, :], all_max[:, :] if KB > 1 else row_max[:, 0, :], -BIG / 2, -1.0,
                                      ALU.max, ALU.mult).then_inc(w.neg_max, 1)

                def max_rows(b):
                    dve.wait_ge(w.max_turned, b.n + 1)
                    dve.tensor_copy(addend[b.side][BK:NM, 0:KB, :],
                                    p_x[0:H, 0:S].unsqueeze(1).to_broadcast([H, KB, S])).then_inc(w.max_copied, 1)

                def residual(b):
                    dve.wait_ge(w.out_mm, b.n + 1)
                    if b.from_(2):
                        dve.wait_ge(w.zn, b.n - 1)
                    dve.tensor_tensor(z[b.side][:, :, :], p_y[:, :].rearrange("p (t d) -> p t d", t=QT),
                                      x_in[b.ring][:, :, :], ALU.add).then_inc(w.z, 1)

                def quotients(b):
                    dve.wait_ge(w.sums_copied, b.n + 1)
                    dve.reciprocal(recips[:, :], sums[:, :]).then_inc(w.recip, 1)
                    dve.wait_ge(w.recip, b.n + 1)
                    if b.from_(1):
                        dve.wait_ge(w.out_mm, b.n)
                    dve.wait_ge(w.pv_copied, b.n + 1)
                    dve.tensor_tensor(attn[:, :], attn_raw[:, :], recips[:, :], ALU.mult).then_inc(w.attn, 1)

                def statistics(b):
                    dve.wait_ge(w.z, b.n + 1)
                    for t in range(QT):
                        last = dve.bn_stats(stats[:, t, :], z[b.side][:, t, :])
                    last.then_inc(w.stats, 1)

                def variance_waits(b):
                    dve.wait_ge(w.stats, b.n + 1)
                    if b.from_(2):
                        dve.wait_ge(w.shift, b.n - 1)

                def variance(b):
                    m = b.side
                    for t in range(QT):
                        last = dve.bn_aggr(moments[m][:, t, :], stats[:, t, :])
                    last.then_inc(w.moments, 1)
                    dve.wait_ge(w.moments, b.n + 1)
                    dve.tensor_scalar(var_eps[m][:, :], moments[m][:, :, 1], EPS, None, ALU.add).then_inc(w.var, 1)

                k_copies(Batch(0, 0))
                q_copies(Batch(0, 0))
                v_copies(Batch(0, 0))
                maxima(Batch(0, 0))

                def slot(i):
                    more = (i + 1).exists(B)
                    if more:
                        k_copies(i + 1)
                    max_rows(i)
                    if i.from_(2):
                        residual(i - 2)
                        statistics(i - 2)
                        variance_waits(i - 2)
                    if more:
                        q_copies(i + 1)
                    if i.from_(2):
                        variance(i - 2)
                    if i.from_(1):
                        quotients(i - 1)
                    if more:
                        v_copies(i + 1)
                        maxima(i + 1)

                slots(dve, slot)
                for b in (Batch(0, B - 2), Batch(0, B - 1)):
                    if b.c == B - 1:
                        quotients(b)
                    residual(b)
                    statistics(b)
                    variance_waits(b)
                    variance(b)

            take_way(dve, program)

        @block.tensor
        def _(pe):
            pe.wait_ge(s_const, N_CONST)
            pe.wait_ge(s_const_r, 1)
            pe.wait_ge(s_look, LOOKS + 1)
            pe.transpose(p_q[0:1, 0:P], least_row[:, :], ident[:, :]).then_inc(s_look_turned, 1)
            pe.wait_ge(s_weights, 64)

            def program(w):
                KB, KS = w.KB, w.KB * BK

                def turn(b):
                    n = b.ring
                    pe.wait_ge(s_x_loaded[n], (b.round + 1) * 16)
                    pe.wait_ge(w.c_loaded[n], (b.round + 1) * 16)
                    pe.wait_ge(w.mask, b.n + 1)
                    if b.from_(2):
                        pe.wait_ge(w.sums_copied, b.n - 1)
                        pe.wait_ge(w.pv_copied, b.n - 1)
                    if b.from_(1):
                        pe.wait_ge(w.v_copied, b.n * KB)
                    for q in range(QT):
                        pe.transpose(p_x[:, q * P:(q + 1) * P], x_in[n][:, q, 0:P], ident[:, :])
                    for kb in range(KB):
                        for q in range(QT):
                            last = pe.transpose(mask_ps[0:BK, kb * S + q * P:kb * S + (q + 1) * P],
                                                mask_b[b.side][:, q, kb * BK:(kb + 1) * BK], ident_b[:, :])
                    last.then_inc(w.m_turned, 1)
                    for t in range(DT):
                        for kb in range(KB):
                            last = pe.transpose(p_k[:, t * KS + kb * BK:t * KS + (kb + 1) * BK],
                                                c_in[n][:, ALL - KB + kb, t * P:(t + 1) * P], ident[0:BK, 0:BK])
                    last.then_inc(w.c_turned, 1)
                    for t in range(1, DT):
                        for q in range(QT):
                            last = pe.transpose(p_x[:, t * S + q * P:t * S + (q + 1) * P],
                                                x_in[n][:, q, t * P:(t + 1) * P], ident[:, :])
                    last.then_inc(w.x_turned, 1)

                def project_k(b):
                    pe.wait_ge(w.c_copied, b.n + 1)
                    for g in range(NG):
                        for t in range(DT):
                            last = pe.matmul(p_k[:, g * KS:(g + 1) * KS], wk_in[:, t, g * P:(g + 1) * P],
                                             cT[:, t, 0:KB, 0, :], start=(t == 0), stop=(t == DT - 1))
                    last.then_inc(w.k_proj, 1)

                def project_q(b):
                    pe.wait_ge(w.x_copied, b.n + 1)
                    if b.from_(1):
                        pe.wait_ge(w.q_copied, b.n)
                    for g in range(NG):
                        for t in range(DT):
                            last = pe.matmul(p_q[:, g * S:(g + 1) * S], wq_in[:, t, g * P:(g + 1) * P], xT[:, t, :],
                                             start=(t == 0), stop=(t == DT - 1))
                    last.then_inc(w.q_proj, 1)

                def project_v(b):
                    pe.wait_ge(w.m_copied, b.n + 1)
                    if b.from_(3):
                        pe.wait_ge(w.z, b.n - 2)
                    for kb in range(KB):
                        if kb:
                            pe.wait_ge(w.v_copied, b.n * KB + kb)
                        for t in range(DT):
                            last = pe.matmul(p_y[:, 0:D], cT[:, t, kb, :, :], wv_sb[:, t, :], start=(t == 0),
                                             stop=(t == DT - 1))
                        last.then_inc(w.v_proj, 1)

                def max_scores(b):
                    m = b.side
                    pe.wait_ge(w.q_rounded, b.n + 1)
                    pe.wait_ge(w.k_hi_spread, b.n + 1)
                    for kb in range(KB):
                        if kb:
                            pe.wait_ge(w.max_red, b.n * KB + kb)
                        for q in range(QT):
                            for g in range(NG):
                                to = sc[:, (q * NG + g) * HG * BK:(q * NG + g + 1) * HG * BK]
                                pe.matmul(to, ident_b[:, :],
                                          mask_b[m][:, q, kb * BK:(kb + 1) * BK].unsqueeze(1)
                                          .to_broadcast([P, HG, BK]), start=True, stop=False)
                                last = pe.matmul(to, q_hi[m][:, g, q * P:(q + 1) * P], k_hi[m][:, kb, g, :, :],
                                                 start=False, stop=True)
                        last.then_inc(w.max_mm, 1)

                def turn_max(b):
                    pe.wait_ge(w.neg_max, b.n + 1)
                    if (b + 1).exists(B):
                        pe.wait_ge(w.x_copied, b.n + 2)
                    else:
                        pe.wait_ge(w.sums_copied, B - 1)
                    for q in range(QT):
                        last = pe.transpose(p_x[0:H, q * P:(q + 1) * P], neg_max[:, q * H:(q + 1) * H], ident[:, :])
                    last.then_inc(w.max_turned, 1)

                def scores(b, kb):
                    m = b.side
                    if kb == 0:
                        pe.wait_ge(w.max_copied, b.n + 1)
                        pe.wait_ge(w.m_copied, b.n + 1)
                        pe.wait_ge(w.k_lo_spread, b.n + 1)
                        pe.wait_ge(w.q_copied, b.n + 1)
                    else:
                        pe.wait_ge(w.exp, b.n * KB + kb)
                    for j in range(NP):
                        to = sc[:, j * S:(j + 1) * S]
                        g, c = j // (NP // NG), j % (NP // NG)
                        hi, lo = (k[m][:, kb, g, 2 * c:2 * c + 2, :] for k in (k_hi, k_lo))
                        pe.matmul(to, spread[:, j, :], addend[m][:, kb, :], start=True, stop=False)
                        pe.matmul(to, lo, q_hi[m][:, g, :], start=False, stop=False)
                        pe.matmul(to, hi, q_lo[m][:, g, :], start=False, stop=False)
                        last = pe.matmul(to, hi, q_hi[m][:, g, :], start=False, stop=True)
                        if j % (NP // 2) == NP // 2 - 1:
                            last.then_inc(w.score[j // (NP // 2)], 1)

                def weigh(b, kb):
                    pe.wait_ge(w.exp, b.n * KB + (kb + 1))
                    pe.wait_ge(w.v_copied, (b.n + 1) * KB)
                    if kb == 0:
                        pe.wait_ge(w.max_copied, b.n + 1)
                        if (b + 1).exists(B):
                            pe.wait_ge(w.k_copied, b.n + 2)
                        else:
                            pe.wait_ge(w.pv_copied, B - 1)
                    for j in range(NP):
                        g, c = j // (NP // NG), j % (NP // NG)
                        last = pe.matmul(p_x[c * PQ:(c + 1) * PQ, g * S:(g + 1) * S], ones_pair[:, :],
                                         probs[:, j, :], start=(kb == 0 and g == 0), stop=(kb == KB - 1),
                                         skip_group_check=True)
                    if kb == KB - 1:
                        last.then_inc(w.sums, 1)
                    for j in range(NP):
                        g, c = j // (NP // NG), j % (NP // NG)
                        last = pe.matmul(p_k[c * PQ:(c + 1) * PQ, g * S:(g + 1) * S], v_pair[b.side][:, kb, j, :],
                                         probs[:, j, :], start=(kb == 0 and g == 0), stop=(kb == KB - 1),
                                         skip_group_check=True)
                    last.then_inc(w.pv, 1)

                def out_project(b):
                    pe.wait_ge(w.attn, b.n + 1)
                    if (b + 3).exists(B):
                        pe.wait_ge(w.m_copied, b.n + 4)
                    if not (b + 3).exists(B):
                        pe.wait_ge(w.v_copied, B * KB)
                    for q in range(QT):
                        for g in range(NG):
                            last = pe.matmul(p_y[:, q * D:(q + 1) * D], attn[:, g * S + q * P:g * S + (q + 1) * P],
                                             wo_sb[:, g, :], start=(g == 0), stop=(g == NG - 1))
                    last.then_inc(w.out_mm, 1)

                def project(b):
                    project_k(b)
                    project_q(b)
                    project_v(b)

                turn(Batch(0, 0))
                project(Batch(0, 0))
                max_scores(Batch(0, 0))

                def slot(i):
                    more = (i + 1).exists(B)
                    if more:
                        turn(i + 1)
                    if i.from_(2):
                        out_project(i - 2)
                    if more:
                        project_k(i + 1)
                    turn_max(i)
                    if more:
                        project_q(i + 1)
                    scores(i, 0)
                    if more:
                        project_v(i + 1)
                    weigh(i, 0)
                    for kb in range(1, KB):
                        scores(i, kb)
                        weigh(i, kb)
                    if more:
                        max_scores(i + 1)

                slots(pe, slot)
                out_project(Batch(0, B - 2))
                pe.wait_ge(w.z, B - 1)
                out_project(Batch(0, B - 1))

            take_way(pe, program)


_INS = ['x', 'ctx_1024', 'mask_BxSxS2_bk1', 'L0_xattn_wq', 'L0_xattn_wk', 'L0_xattn_wv', 'L0_xattn_wo',
        'L0_xattn_gamma', 'L0_xattn_beta']


def kernel(**inputs):
    import numpy as np
    import concourse.bacc as bacc
    from concourse.bass_utils import run_bass_kernel_spmd

    nc = bacc.Bacc("TRN2", target_bir_lowering=False, num_devices=1)
    arrays, args = {}, []
    for name in _INS:
        a = np.ascontiguousarray(inputs[name])
        arrays[name] = a
        args.append(nc.dram_tensor(name, a.shape, mybir.dt.from_np(a.dtype), kind="ExternalInput").ap())
    shape = inputs['x'].shape
    out = nc.dram_tensor("out", shape, F32, kind="ExternalOutput").ap()
    build(nc, *args, out)
    r = run_bass_kernel_spmd(nc, [arrays], core_ids=[0])
    return r.results[0]["out"]
```

```python
import concourse.bass as bass
from concourse import mybir
from contextlib import ExitStack

F32 = mybir.dt.float32
F32R = mybir.dt.float32r
BF16 = mybir.dt.bfloat16
U8 = mybir.dt.uint8
U16 = mybir.dt.uint16
I32 = mybir.dt.int32
ACT = mybir.ActivationFunctionType
ALU = mybir.AluOpType
AX = mybir.AxisListType

P = 128
BIG = 2.0 ** 100
EPS = 1e-5
N_CONST = 14
N_CONST_A = 5
UNROLL = 4
PEEL = 6


class Batch:

    def __init__(self, t, c):
        self.t, self.c = t, c
        self.n = c if isinstance(t, int) and t == 0 else t * UNROLL + c
        self.ring = c % UNROLL
        self.side = c % 2
        self.round = c // UNROLL if isinstance(t, int) else t + c // UNROLL
        self.turn = c // 2 if isinstance(t, int) else t * (UNROLL // 2) + c // 2

    def __add__(self, n):
        return Batch(self.t, self.c + n)

    def __sub__(self, n):
        return Batch(self.t, self.c - n)

    def from_(self, n):
        return self.c >= n

    def exists(self, batches):
        return not isinstance(self.t, int) or self.c < batches


def build(nc, x, ctx_in, mask, wq, wk, wv, wo, gamma, beta, out):
    B, S, D = x.shape
    SK = ctx_in.shape[1]
    H, HD = 16, 16
    SCALE = float(HD) ** -0.5
    QT = S // P
    DT = D // P
    BK = 64
    ALL = SK // BK
    HG = P // HD
    NG = H // HG
    NP = H // 2
    PQ = 32
    LOOKS = 4
    HH = HG // 2
    HALF = [slice(0, BK), slice(BK, P)]

    ctx = ExitStack()
    with ctx:
        def sb(name, shape, dt=F32):
            return ctx.enter_context(nc.sbuf_tensor(name, shape, dt))

        def pb(name, shape, dt=F32):
            return ctx.enter_context(nc.psum_tensor(name, shape, dt))

        def sem(name):
            return ctx.enter_context(nc.semaphore(name))

        ident = sb("ident", [P, P])
        ident_b = sb("ident_b", [P, P], BF16)
        head_rows = sb("head_rows", [P, HG])
        head_of_key = sb("head_of_key", [P, NG, HH, BK])
        zeros = sb("zeros", [P, NG * S])
        ones_pair = sb("ones_pair", [P, PQ])
        half_neg = sb("half_neg", [P, QT])
        neg_one = sb("neg_one", [P, QT])
        wq_in = sb("wq_in", [P, DT, D])
        wq_hi = sb("wq_hi", [P, DT, D], F32R)
        wq_lo = sb("wq_lo", [P, DT, D], F32R)
        wk_in = sb("wk_in", [P, DT, D])
        wv_sb = sb("wv_sb", [P, DT, D])
        wo_sb = sb("wo_sb", [P, DT, D])
        gamma_sb = sb("gamma_sb", [P, D])
        beta_sb = sb("beta_sb", [P, D])
        x_in = [sb(f"x_in{n}", [P, QT, D]) for n in range(UNROLL)]
        c_in = sb("c_in", [P, UNROLL * ALL // 2, D])
        m_in = sb("m_in", [P, B * QT, SK], U8)
        mask_b = [sb(f"mask_b{n}", [P, QT, ALL, 2, BK], BF16) for n in range(2)]
        x_hi = sb("x_hi", [P, DT, S], F32R)
        x_lo = sb("x_lo", [P, DT, S], F32R)
        cT = sb("cT", [P, DT, ALL * BK])
        q_mask = [[sb(f"q_mask{h}{n}", [P, ALL, NG, S], F32R) for n in range(2)] for h in range(2)]
        q_max = [[sb(f"q_max{h}{n}", [P, NG, S], F32R) for n in range(2)] for h in range(2)]
        q_rest = [[sb(f"q_rest{h}{n}", [P, NG, S], F32R) for n in range(2)] for h in range(2)]
        kT_hi = sb("kT_hi", [P, NG, ALL, BK], F32R)
        kT_lo = sb("kT_lo", [P, NG, ALL, BK], F32R)
        k_hi = sb("k_hi", [P, ALL, NG, HG, BK], F32R)
        k_lo = sb("k_lo", [P, ALL, NG, HG, BK], F32R)
        v_pair = sb("v_pair", [P, 2 * ALL, NP, PQ])
        row_max = sb("row_max", [P, ALL, QT * H])
        all_max = sb("all_max", [P, QT * H])
        neg_max = sb("neg_max", [P, QT, 2, BK])
        probs = sb("probs", [P, NP, S])
        sums = sb("sums", [P, NG * S])
        recips = sb("recips", [P, NG * S])
        attn_raw = sb("attn_raw", [P, NG * S])
        attn = sb("attn", [P, NG * S])
        z = [sb(f"z{n}", [P, QT, D]) for n in range(2)]
        stats = sb("stats", [P, QT, 6])
        moments = [sb(f"moments{n}", [P, QT, 2]) for n in range(2)]
        var_eps = [sb(f"var_eps{n}", [P, QT]) for n in range(2)]
        rstd = [sb(f"rstd{n}", [P, QT]) for n in range(2)]
        mu_rstd = [sb(f"mu_rstd{n}", [P, QT]) for n in range(2)]
        shift = [sb(f"shift{n}", [P, QT]) for n in range(2)]
        zn = [sb(f"zn{n}", [P, QT, D]) for n in range(2)]
        zg = sb("zg", [P, QT, D])
        zg_last = sb("zg_last", [P, QT, D])
        y = [sb(f"y{n}", [P, QT, D]) for n in range(2)]
        least = sb("least", [P, LOOKS])
        least_row = sb("least_row", [P, 1])
        least_all = sb("least_all", [1, 1])
        one_block = sb("one_block", [1, 1], I32)
        sc = pb("sc", [P, NP * S])
        p_x = pb("p_x", [P, 512])
        p_q = pb("p_q", [P, 512])
        p_y = pb("p_y", [P, 512])
        p_k = pb("p_k", [P, 512])
        mask_ps = p_q[:, :].bitcast(BF16)

        s_const = sem("s_const")
        s_const_r = sem("s_const_r")
        s_const_k = sem("s_const_k")
        s_weights = [sem(f"s_weights{n}") for n in range(4)]
        s_split = sem("s_split")
        s_affine = sem("s_affine")
        s_mask_in = [sem(f"s_mask_in{n}") for n in range(LOOKS)]
        s_zeros = sem("s_zeros")
        s_look = sem("s_look")
        s_look_turned = sem("s_look_turned")
        s_one_block = sem("s_one_block")
        s_x_loaded = [sem(f"s_x_loaded{n}") for n in range(UNROLL)]

        class Way:

            def __init__(self, name, blocks):
                def sem_(what):
                    return sem(f"{name}_{what}")

                self.KB = blocks
                self.K0 = SK - blocks * BK
                self.TILES = (blocks + 1) // 2
                self.PB = 2 * self.TILES // blocks
                self.c_loaded = [sem_(f"c_loaded{n}") for n in range(UNROLL)]
                self.mask = sem_("mask")
                self.x_turned = sem_("x_turned")
                self.c_turned = sem_("c_turned")
                self.m_turned = sem_("m_turned")
                self.x_rounded = sem_("x_rounded")
                self.x_copied = sem_("x_copied")
                self.c_copied = sem_("c_copied")
                self.m_copied = sem_("m_copied")
                self.k_proj = sem_("k_proj")
                self.q_proj = sem_("q_proj")
                self.v_proj = sem_("v_proj")
                self.k_rounded = sem_("k_rounded")
                self.k_copied = sem_("k_copied")
                self.k_hi_spread = sem_("k_hi_spread")
                self.k_lo_spread = sem_("k_lo_spread")
                self.q_rounded = sem_("q_rounded")
                self.q_copied = sem_("q_copied")
                self.q_rest = sem_("q_rest")
                self.v_copied = sem_("v_copied")
                self.max_mm = [sem_(f"max_mm{n}") for n in range(QT)]
                self.max_red = sem_("max_red")
                self.all_max = sem_("all_max")
                self.neg_max = sem_("neg_max")
                self.max_turned = sem_("max_turned")
                self.max_copied = sem_("max_copied")
                self.score = [sem_(f"score{n}") for n in range(2)]
                self.exp = [sem_(f"exp{n}") for n in range(2)]
                self.sums = sem_("sums")
                self.pv = sem_("pv")
                self.sums_copied = sem_("sums_copied")
                self.pv_copied = sem_("pv_copied")
                self.recip = sem_("recip")
                self.attn = sem_("attn")
                self.out_mm = sem_("out_mm")
                self.z = sem_("z")
                self.stats = sem_("stats")
                self.moments = sem_("moments")
                self.var = sem_("var")
                self.rstd = sem_("rstd")
                self.mu_rstd = sem_("mu_rstd")
                self.shift = sem_("shift")
                self.zn = sem_("zn")
                self.zg = sem_("zg")
                self.y = sem_("y")
                self.zg_last = sem_("zg_last")
                self.y_last = sem_("y_last")
                self.stored = [sem_(f"stored{n}") for n in range(2)]

            def leads(self, b):
                return self.PB == 1 or b.side == 0

            def tiles(self, b):
                return (b.n if self.PB == 1 else b.turn) + 1

            def tile(self, b):
                return b.ring * self.TILES // self.PB

            def blk(self, b, kb):
                return b.side if self.PB == 2 else kb

        last_block, all_blocks = Way("last", 1), Way("all", ALL)

        block = ctx.enter_context(nc.Block())

        def slots(eng, slot):
            loops = (B - PEEL - 2) // UNROLL
            for i in range(PEEL):
                slot(Batch(0, i))
            with eng.Fori(0, loops) as t:
                for u in range(UNROLL):
                    slot(Batch(t, PEEL + u))
            for i in range(PEEL + loops * UNROLL, B):
                slot(Batch(0, i))

        def take_way(eng, steps, rest_of_last):
            eng.wait_ge(s_one_block, 1)
            found = eng.value_load(one_block[0:1, 0:1], min_val=0, max_val=1)
            with eng.If(found != 0):
                rest_of_last()
            with eng.Else():
                eng.wait_ge(last_block.k_lo_spread, 1)
                eng.wait_ge(last_block.v_copied, 1)
                eng.wait_ge(last_block.q_rest, 1)
                eng.wait_ge(last_block.q_copied, 2)
                first, rest = steps(all_blocks)
                for step in first:
                    step()
                rest()

        @block.sync
        def _(sp):
            x_v = x.rearrange("b (p t) d -> b p t d", t=QT)
            o_v = out.rearrange("b (p t) d -> b p t d", t=QT)

            def load_x(b):
                sp.dma_start(x_in[b.ring][:, :, :],
                             x_v[bass.ds(b.n, 1), :, :, :].squeeze(0)).then_inc(s_x_loaded[b.ring], 16)

            def load_weights(n, to, d):
                sp.dma_start(to[:, :, :], d.rearrange("(t p) n -> p t n", p=P)).then_inc(s_weights[n], 16)

            load_weights(0, wq_in, wq)
            load_x(Batch(0, 0))

            def steps(w):
                c_v = ctx_in.rearrange("(m n) (t p) d -> m n p t d", n=w.PB, p=P)

                def load_ctx(b):
                    if b.from_(UNROLL):
                        sp.wait_ge(w.c_turned, w.tiles(b) - UNROLL // w.PB)
                    for n in range(w.PB):
                        rows = HALF[n] if w.PB == 2 else slice(0, P)
                        sp.dma_start(c_in[rows, w.tile(b):w.tile(b) + w.TILES, :],
                                     c_v[bass.ds(w.tiles(b) - 1, 1), n, (BK if w.PB == 2 else 0):, w.K0 // P:, :]
                                     .squeeze(0)).then_inc(w.c_loaded[b.ring], 16)

                def store(b):
                    if b.c == B - 1:
                        sp.wait_ge(w.y_last, 1)
                    else:
                        sp.wait_ge(w.y, b.n + 1)
                    sp.dma_start(o_v[bass.ds(b.n, 1), :, :, :].squeeze(0),
                                 y[b.side][:, :, :]).then_inc(w.stored[b.side], 16)

                def slot(i):
                    if w.leads(i) and i.from_(1):
                        load_ctx(i)
                    if i.from_(UNROLL):
                        sp.wait_ge(w.z, i.n - (UNROLL - 1))
                        load_x(i)
                    if i.from_(UNROLL + 1):
                        store(i - (UNROLL + 1))

                def rest():
                    slots(sp, slot)
                    for b in range(B - UNROLL - 1, B):
                        store(Batch(0, b))
                    for n in range(2):
                        sp.wait_ge(w.stored[n], 16 * (B // 2))

                return [lambda: load_ctx(Batch(0, 0))], rest

            (first_ctx,), rest = steps(last_block)
            first_ctx()
            load_weights(1, wk_in, wk)
            load_weights(2, wv_sb, wv)
            load_weights(3, wo_sb, wo)
            for i in range(1, UNROLL):
                load_x(Batch(0, i))
            take_way(sp, steps, rest)

        @block.gpsimd
        def _(pool):
            made = [0]

            def step(ins):
                made[0] += 1
                ins.then_inc(s_const, 1)
                pool.wait_ge(s_const, made[0])

            step(pool.memset(ident[:, :], 0.0))
            step(pool.affine_select(out=ident[:, :], in_=ident[:, :], compare_op=ALU.not_equal, fill=1.0, base=0,
                                    pattern=[[-1, P]], channel_multiplier=1))
            step(pool.memset(head_of_key[:, :, :, :], 0.0))
            for half in range(2):
                v = head_of_key[(1 - half) * BK:(1 - half) * BK + H, :, :, :]
                step(pool.affine_select(out=v, in_=v, compare_op=ALU.not_equal, fill=1.0, base=-half * HH,
                                        pattern=[[-HG, NG], [-1, HH], [0, BK]], channel_multiplier=1))
            step(pool.memset(head_rows[:, :], 1.0))
            step(pool.affine_select(out=head_rows[:, :], in_=head_rows[:, :], compare_op=ALU.is_ge, fill=0.0, base=0,
                                    pattern=[[-HD, HG]], channel_multiplier=1))
            step(pool.affine_select(out=head_rows[:, :], in_=head_rows[:, :], compare_op=ALU.is_ge, fill=0.0,
                                    base=HD - 1, pattern=[[HD, HG]], channel_multiplier=-1))
            step(pool.memset(ones_pair[:, :], 0.0))
            for half in range(2):
                step(pool.memset(ones_pair[half * BK:(half + 1) * BK, half * HD:(half + 1) * HD], 1.0))
            step(pool.memset(half_neg[:, :], -0.5))
            step(pool.memset(neg_one[:, :], -1.0))
            step(pool.memset(v_pair[:, :, :, :], 0.0))
            pool.wait_ge(s_affine, 32)

            def steps(w):
                KB = w.KB

                def spread(b, kT, to, copied, spread_):
                    pool.wait_ge(copied, w.tiles(b))
                    if b.from_(w.PB):
                        pool.wait_ge(w.exp[1], (b.n + 1 - w.PB) * KB)
                    for kb in range(KB):
                        n = w.blk(b, kb)
                        for half in range(2):
                            r, heads = HALF[half], slice(half * HH, (half + 1) * HH)
                            last = pool.tensor_tensor(
                                to[r, n, :, heads, :],
                                kT[r, :, n, :].bitcast(F32).unsqueeze(2).to_broadcast([BK, NG, HH, BK]),
                                head_rows[r, heads].unsqueeze(1).unsqueeze(3).to_broadcast([BK, NG, HH, BK]),
                                ALU.mult)
                            if half == 1:
                                last.then_inc(spread_, 1)
                                pool.wait_ge(spread_, b.n * KB + (kb + 1))

                def spread_hi(b):
                    spread(b, kT_hi, k_hi, w.k_rounded, w.k_hi_spread)

                def spread_lo(b):
                    spread(b, kT_lo, k_lo, w.k_copied, w.k_lo_spread)

                def quotients(b):
                    pool.wait_ge(w.recip, b.n + 1)
                    if b.from_(1):
                        pool.wait_ge(w.out_mm, b.n)
                    pool.wait_ge(w.pv_copied, b.n + 1)
                    pool.tensor_tensor(attn[:, :], attn_raw[:, :], recips[:, :], ALU.mult).then_inc(w.attn, 1)
                    pool.wait_ge(w.attn, b.n + 1)

                def scales(b):
                    m = b.side
                    pool.wait_ge(w.var, b.n + 1)
                    if b.from_(2):
                        pool.wait_ge(w.zn, b.n - 1)
                    pool.tensor_tensor(rstd[m][:, :], var_eps[m][:, :], half_neg[:, :], ALU.pow).then_inc(w.rstd, 1)
                    pool.wait_ge(w.rstd, b.n + 1)
                    pool.tensor_tensor(mu_rstd[m][:, :], moments[m][:, :, 0], rstd[m][:, :],
                                       ALU.mult).then_inc(w.mu_rstd, 1)
                    pool.wait_ge(w.mu_rstd, b.n + 1)
                    pool.tensor_tensor(shift[m][:, :], mu_rstd[m][:, :], neg_one[:, :], ALU.mult).then_inc(w.shift, 1)
                    pool.wait_ge(w.shift, b.n + 1)

                def affine(b):
                    m = b.side
                    pool.wait_ge(w.zn, b.n + 1)
                    pool.tensor_tensor(zg[:, :, :], zn[m][:, :, :],
                                       gamma_sb[:, :].unsqueeze(1).to_broadcast([P, QT, D]),
                                       ALU.mult).then_inc(w.zg, 1)
                    pool.wait_ge(w.zg, b.n + 1)
                    if b.from_(2):
                        pool.wait_ge(w.stored[m], b.turn * 16)
                    pool.tensor_tensor(y[m][:, :, :], zg[:, :, :],
                                       beta_sb[:, :].unsqueeze(1).to_broadcast([P, QT, D]),
                                       ALU.add).then_inc(w.y, 1)
                    pool.wait_ge(w.y, b.n + 1)

                def slot(i):
                    more = (i + 1).exists(B)
                    if more and not w.leads(i + 1):
                        spread_hi(i + 1)
                    if i.from_(3):
                        affine(i - 3)
                    if more and w.leads(i + 1):
                        spread_hi(i + 1)
                    if i.from_(1):
                        quotients(i - 1)
                    if more:
                        spread_lo(i + 1)
                    if i.from_(2):
                        scales(i - 2)

                def rest():
                    slots(pool, slot)
                    affine(Batch(0, B - 3))
                    for b in range(B - 2, B):
                        scales(Batch(0, b))
                    affine(Batch(0, B - 2))

                return [lambda: spread_hi(Batch(0, 0)), lambda: spread_lo(Batch(0, 0))], rest

            first, rest = steps(last_block)
            for step_ in first:
                step_()
            take_way(pool, steps, rest)

        @block.scalar
        def _(act):
            m_v = mask.rearrange("b (p t) k -> p b t k", t=QT)
            for n in range(LOOKS):
                r = slice(n * B // LOOKS, (n + 1) * B // LOOKS)
                act.dma_start(m_in[:, r.start * QT:r.stop * QT, :].rearrange("p (b t) k -> p b t k", t=QT),
                              m_v[:, r, :, :]).then_inc(s_mask_in[n], 16)
            act.dma_start(gamma_sb[:, :], gamma.partition_broadcast(P)).then_inc(s_affine, 16)
            act.dma_start(beta_sb[:, :], beta.partition_broadcast(P)).then_inc(s_affine, 16)
            act.wait_ge(s_mask_in[0], 16)

            def steps(w):
                KB = w.KB

                def rows_beside_k(n):
                    for half in range(2):
                        r, heads = HALF[1 - half], slice(half * HH, (half + 1) * HH)
                        act.activation(k_hi[r, n, :, heads, :],
                                       ident[r, r].unsqueeze(1).unsqueeze(2).to_broadcast([BK, NG, HH, BK]), ACT.Copy)
                        last = act.activation(k_lo[r, n, :, heads, :], head_of_key[r, :, :, :], ACT.Copy)
                    last.then_inc(s_const_k, 1)

                def mask_addend(b):
                    for t in range(QT):
                        last = act.activation(
                            mask_b[b.side][:, t, 0:KB, :, :],
                            m_in[:, bass.ds(b.n * QT + t, 1), w.K0:].squeeze(1).rearrange("p (k c) -> p k c", k=KB)
                            .unsqueeze(2).to_broadcast([P, KB, 2, BK]), ACT.Copy, scale=-BIG)
                    last.then_inc(w.mask, 1)

                def copies(b):
                    act.wait_ge(w.x_turned, b.n + 1)
                    if b.from_(1):
                        act.wait_ge(w.q_proj, b.n)
                    act.activation(x_hi[:, :, :], p_x[:, :].rearrange("p (t s) -> p t s", t=DT),
                                   ACT.Copy).then_inc(w.x_rounded, 1)
                    if w.leads(b):
                        act.wait_ge(w.c_turned, w.tiles(b))
                        act.activation(cT[:, :, 0:w.TILES * P],
                                       p_k[:, 0:DT * w.TILES * P].rearrange("p (t c) -> p t c", t=DT),
                                       ACT.Copy).then_inc(w.c_copied, 1)
                    act.wait_ge(w.m_turned, b.n + 1)
                    for half in range(2):
                        r = HALF[1 - half]
                        for g in range(NG):
                            last = act.activation(q_mask[half][b.side][r, 0:KB, g, :],
                                                  mask_ps[r, 0:KB * S].rearrange("p (k s) -> p k s", k=KB), ACT.Copy)
                    last.then_inc(w.m_copied, 1)

                def round_q(b):
                    act.wait_ge(w.q_proj, b.n + 1)
                    for half in range(2):
                        r = HALF[half]
                        for kb in range(KB):
                            last = act.activation(q_mask[half][b.side][r, kb, :, :],
                                                  p_q[r, :].rearrange("p (g s) -> p g s", g=NG), ACT.Copy)
                    last.then_inc(w.q_rounded, 1)

                def copy_q(b, half):
                    act.wait_ge(w.q_rounded, b.n + 1)
                    r = HALF[half]
                    act.activation(q_max[half][b.side][r, :, :], q_mask[half][b.side][r, 0, :, :].bitcast(F32),
                                   ACT.Copy).then_inc(w.q_copied, 1)

                def max_rows(b):
                    act.wait_ge(w.max_turned, b.n + 1)
                    for half in range(2):
                        r = slice((1 - half) * BK, (1 - half) * BK + H)
                        last = act.activation(q_max[half][b.side][r, :, :],
                                              sc[r, 0:S].unsqueeze(1).to_broadcast([H, NG, S]), ACT.Copy)
                    last.then_inc(w.max_copied, 1)

                def v_copies(b):
                    act.wait_ge(w.v_proj, w.tiles(b))
                    if w.PB == 2 and b.from_(4):
                        act.wait_ge(w.pv, b.n - 2)
                    for t in range(w.TILES):
                        for n in range(2):
                            to = b.ring + n if w.PB == 2 else b.side * ALL + 2 * t + n
                            for half in range(2):
                                last = act.activation(
                                    v_pair[HALF[half], to, :, half * HD:(half + 1) * HD],
                                    p_y[HALF[n], t * D:(t + 1) * D]
                                    .rearrange("p (j h d) -> p j h d", h=2, d=HD)[:, :, half, :], ACT.Copy)
                    last.then_inc(w.v_copied, 1)

                def exps(b, kb, a):
                    half = NP // 2
                    act.wait_ge(w.score[a], b.n * KB + (kb + 1))
                    act.activation(
                        probs[:, a * half:(a + 1) * half, :],
                        sc[:, a * half * S:(a + 1) * half * S].rearrange("p (j s) -> p j s", j=half),
                        ACT.Exp, scale=SCALE).then_inc(w.exp[a], 1)

                def attn_copies(b):
                    act.wait_ge(w.sums, b.n + 1)
                    if b.from_(1):
                        act.wait_ge(w.attn, b.n)
                    act.activation(sums[:, :], p_x[:, :], ACT.Copy).then_inc(w.sums_copied, 1)
                    act.wait_ge(w.pv, (b.n + 1) * KB)
                    act.activation(attn_raw[:, :], p_k[:, :], ACT.Copy).then_inc(w.pv_copied, 1)

                def normalise(b):
                    m = b.side
                    act.wait_ge(w.shift, b.n + 1)
                    if b.from_(2):
                        act.wait_ge(w.zg, b.n - 1)
                    for t in range(QT):
                        last = act.activation(zn[m][:, t, :], z[m][:, t, :], ACT.Identity, bias=shift[m][:, t:t + 1],
                                              scale=rstd[m][:, t:t + 1])
                    last.then_inc(w.zn, 1)

                def slot(i):
                    more = (i + 1).exists(B)
                    if more:
                        copies(i + 1)
                    if i.from_(3):
                        normalise(i - 3)
                    max_rows(i)
                    if (i + 2).exists(B):
                        mask_addend(i + 2)
                    if more:
                        round_q(i + 1)
                    for a in range(2):
                        exps(i, 0, a)
                        if more:
                            copy_q(i + 1, a)
                    if more and w.leads(i + 1):
                        v_copies(i + 1)
                    for kb in range(1, KB):
                        for a in range(2):
                            exps(i, kb, a)
                    attn_copies(i)

                def first():
                    mask_addend(Batch(0, 0))
                    mask_addend(Batch(0, 1))
                    if w is last_block:
                        act.wait_ge(s_const, N_CONST_A)
                        rows_beside_k(0)
                    else:
                        for n in range(2, ALL):
                            rows_beside_k(n)
                    copies(Batch(0, 0))
                    if w is last_block:
                        rows_beside_k(1)
                    round_q(Batch(0, 0))
                    for half in range(2):
                        copy_q(Batch(0, 0), half)
                    v_copies(Batch(0, 0))

                def rest():
                    slots(act, slot)
                    for b in range(B - 3, B):
                        normalise(Batch(0, b))

                return [first], rest

            (first,), rest = steps(last_block)
            first()
            for n in range(1, LOOKS):
                act.wait_ge(s_mask_in[n], 16)
            take_way(act, steps, rest)

        @block.vector
        def _(dve):
            dve.memset(zeros[:, :], 0.0).then_inc(s_zeros, 1)
            dve.wait_ge(s_zeros, 1)
            for n in range(2):
                for half in range(2):
                    r = HALF[1 - half]
                    dve.tensor_copy(q_max[half][n][r, :, :], zeros[r, :].rearrange("p (g s) -> p g s", g=NG))
                    dve.tensor_copy(q_rest[half][n][r, :, :],
                                    zeros[r, :].rearrange("p (g s) -> p g s", g=NG))
            dve.tensor_copy(neg_max[:, :, :, :], zeros[:, 0:QT * P].rearrange("p (q n c) -> p q n c", q=QT, n=2))
            dve.wait_ge(s_const, N_CONST_A)
            dve.tensor_copy(ident_b[:, :], ident[:, :]).then_inc(s_const_r, 1)

            def steps(w):
                KB = w.KB

                def k_copies(b):
                    dve.wait_ge(w.k_proj, w.tiles(b))
                    if b.from_(1):
                        dve.wait_ge(w.k_lo_spread, b.n * KB)
                    n = 2 * w.TILES
                    ps = p_k[:, 0:NG * n * BK].rearrange("p (g k c) -> p g k c", g=NG, k=n)
                    hi, lo = kT_hi[:, :, 0:n, :], kT_lo[:, :, 0:n, :]
                    dve.tensor_copy(hi, ps).then_inc(w.k_rounded, 1)
                    dve.wait_ge(w.k_rounded, w.tiles(b))
                    dve.tensor_tensor(lo, ps, hi.bitcast(F32), ALU.subtract).then_inc(w.k_copied, 1)

                def x_rest(b):
                    if b.from_(1):
                        dve.wait_ge(w.q_proj, b.n)
                    dve.wait_ge(w.x_rounded, b.n + 1)
                    dve.tensor_tensor(x_lo[:, :, :], p_x[:, :].rearrange("p (t s) -> p t s", t=DT),
                                      x_hi[:, :, :].bitcast(F32), ALU.subtract).then_inc(w.x_copied, 1)

                def q_rests(b):
                    dve.wait_ge(w.q_rounded, b.n + 1)
                    for half in range(2):
                        r = HALF[half]
                        last = dve.tensor_tensor(q_rest[half][b.side][r, :, :],
                                                 p_q[r, :].rearrange("p (g s) -> p g s", g=NG),
                                                 q_mask[half][b.side][r, 0, :, :].bitcast(F32), ALU.subtract)
                    last.then_inc(w.q_rest, 1)

                def maxima(b):
                    for kb in range(KB):
                        for q in range(QT):
                            dve.wait_ge(w.max_mm[q], b.n * KB + (kb + 1))
                            last = dve.tensor_reduce(
                                row_max[:, kb, q * H:(q + 1) * H],
                                sc[:, q * H * BK:(q + 1) * H * BK].rearrange("p (r c) -> p r c", c=BK), AX.X, ALU.max)
                        last.then_inc(w.max_red, 1)
                    dve.wait_ge(w.max_red, (b.n + 1) * KB)
                    if KB > 1:
                        dve.tensor_reduce(all_max[:, :], row_max[:, :, :].rearrange("p k r -> p r k"), AX.X,
                                          ALU.max).then_inc(w.all_max, 1)
                        dve.wait_ge(w.all_max, b.n + 1)
                    dve.tensor_scalar(neg_max[:, :, :, 0:H],
                                      (all_max[:, :] if KB > 1 else row_max[:, 0, :])
                                      .rearrange("p (q h) -> p q h", h=H).unsqueeze(2).to_broadcast([P, QT, 2, H]),
                                      -BIG / 2, -1.0, ALU.max, ALU.mult).then_inc(w.neg_max, 1)

                def residual(b):
                    dve.wait_ge(w.out_mm, b.n + 1)
                    if b.from_(2):
                        dve.wait_ge(w.zn, b.n - 1)
                    dve.tensor_tensor(z[b.side][:, :, :], p_y[:, :].rearrange("p (t d) -> p t d", t=QT),
                                      x_in[b.ring][:, :, :], ALU.add).then_inc(w.z, 1)

                def reciprocals(b, half):
                    c = slice(half * S, (half + 1) * S)
                    if half == 0:
                        dve.wait_ge(w.sums_copied, b.n + 1)
                        if b.from_(1):
                            dve.wait_ge(w.attn, b.n)
                    last = dve.reciprocal(recips[:, c], sums[:, c])
                    if half == 1:
                        last.then_inc(w.recip, 1)

                def last_quotients(b):
                    dve.wait_ge(w.recip, b.n + 1)
                    dve.wait_ge(w.out_mm, b.n)
                    dve.wait_ge(w.pv_copied, b.n + 1)
                    dve.tensor_tensor(attn[:, :], attn_raw[:, :], recips[:, :], ALU.mult).then_inc(w.attn, 1)

                def statistics(b):
                    dve.wait_ge(w.z, b.n + 1)
                    for t in range(QT):
                        last = dve.bn_stats(stats[:, t, :], z[b.side][:, t, :])
                    last.then_inc(w.stats, 1)

                def variance_waits(b):
                    dve.wait_ge(w.stats, b.n + 1)
                    if b.from_(2):
                        dve.wait_ge(w.shift, b.n - 1)

                def variance(b):
                    m = b.side
                    for t in range(QT):
                        last = dve.bn_aggr(moments[m][:, t, :], stats[:, t, :])
                    last.then_inc(w.moments, 1)
                    dve.wait_ge(w.moments, b.n + 1)
                    dve.tensor_scalar(var_eps[m][:, :], moments[m][:, :, 1], EPS, None, ALU.add).then_inc(w.var, 1)

                def slot(i):
                    more = (i + 1).exists(B)
                    if more:
                        x_rest(i + 1)
                    if i.from_(1):
                        reciprocals(i - 1, 0)
                    if more and w.leads(i + 1):
                        k_copies(i + 1)
                    if i.from_(2):
                        residual(i - 2)
                        statistics(i - 2)
                        variance_waits(i - 2)
                    if i.from_(1):
                        reciprocals(i - 1, 1)
                    if i.from_(2):
                        variance(i - 2)
                    if more:
                        q_rests(i + 1)
                        maxima(i + 1)

                def last_affine(b):
                    dve.wait_ge(s_affine, 32)
                    dve.wait_ge(w.zn, b.n + 1)
                    dve.tensor_tensor(zg_last[:, :, :], zn[b.side][:, :, :],
                                      gamma_sb[:, :].unsqueeze(1).to_broadcast([P, QT, D]),
                                      ALU.mult).then_inc(w.zg_last, 1)
                    dve.wait_ge(w.stored[b.side], b.turn * 16)
                    dve.wait_ge(w.zg_last, 1)
                    dve.tensor_tensor(y[b.side][:, :, :], zg_last[:, :, :],
                                      beta_sb[:, :].unsqueeze(1).to_broadcast([P, QT, D]),
                                      ALU.add).then_inc(w.y_last, 1)

                def rest():
                    maxima(Batch(0, 0))
                    slots(dve, slot)
                    reciprocals(Batch(0, B - 1), 0)
                    reciprocals(Batch(0, B - 1), 1)
                    last_quotients(Batch(0, B - 1))
                    for b in (Batch(0, B - 2), Batch(0, B - 1)):
                        residual(b)
                        statistics(b)
                        variance_waits(b)
                        variance(b)
                    last_affine(Batch(0, B - 1))

                return [lambda: x_rest(Batch(0, 0)), lambda: k_copies(Batch(0, 0)),
                        lambda: q_rests(Batch(0, 0))], rest

            def look(n):
                r = slice(n * B * QT // LOOKS, (n + 1) * B * QT // LOOKS)
                dve.wait_ge(s_mask_in[n], 16)
                dve.tensor_reduce(least[:, n:n + 1], m_in[:, r, 0:SK - BK].bitcast(U16), AX.XY,
                                  ALU.min).then_inc(s_look, 1)

            first, rest = steps(last_block)
            look(0)
            dve.wait_ge(s_weights[0], 16)
            dve.tensor_copy(wq_hi[:, :, :], wq_in[:, :, :]).then_inc(s_split, 1)
            dve.wait_ge(s_split, 1)
            dve.tensor_tensor(wq_lo[:, :, :], wq_in[:, :, :], wq_hi[:, :, :].bitcast(F32),
                              ALU.subtract).then_inc(s_split, 1)
            look(1)
            x_rest, k_copies, q_rests = first
            x_rest()
            look(2)
            k_copies()
            look(3)
            dve.wait_ge(s_look, LOOKS)
            dve.tensor_reduce(least_row[:, :], least[:, :], AX.X, ALU.min).then_inc(s_look, 1)
            q_rests()
            dve.wait_ge(s_look_turned, 1)
            dve.tensor_reduce(least_all[:, :], sc[0:1, 0:P], AX.X, ALU.min).then_inc(s_look, 1)
            dve.wait_ge(s_look, LOOKS + 2)
            dve.tensor_scalar(one_block[:, :], least_all[:, :], 257.0, None, ALU.is_ge).then_inc(s_one_block, 1)

            take_way(dve, steps, rest)

        @block.tensor
        def _(pe):
            pe.wait_ge(s_const, N_CONST)
            pe.wait_ge(s_const_r, 1)
            pe.wait_ge(s_split, 2)

            def steps(w):
                KB, TK = w.KB, w.TILES * P

                def turn(b):
                    n = b.ring
                    pe.wait_ge(s_x_loaded[n], (b.round + 1) * 16)
                    if w.leads(b):
                        pe.wait_ge(w.c_loaded[n], (b.round + 1) * (16 * w.PB))
                    pe.wait_ge(w.mask, b.n + 1)
                    if b.from_(1):
                        pe.wait_ge(w.q_rest, b.n)
                    if b.from_(2):
                        pe.wait_ge(w.sums_copied, b.n - 1)
                    for t in range(DT):
                        for q in range(QT):
                            last = pe.transpose(p_x[:, t * S + q * P:t * S + (q + 1) * P],
                                                x_in[n][:, q, t * P:(t + 1) * P], ident[:, :])
                    last.then_inc(w.x_turned, 1)
                    if w.leads(b):
                        if b.from_(2):
                            pe.wait_ge(w.pv_copied, b.n - 1)
                        for t in range(DT):
                            for k in range(w.TILES):
                                last = pe.transpose(p_k[:, t * TK + k * P:t * TK + (k + 1) * P],
                                                    c_in[:, w.tile(b) + k, t * P:(t + 1) * P], ident[:, :])
                        last.then_inc(w.c_turned, 1)
                    for kb in range(KB):
                        for q in range(QT):
                            last = pe.transpose(mask_ps[:, kb * S + q * P:kb * S + (q + 1) * P],
                                                mask_b[b.side][:, q, kb, :, :], ident_b[:, :])
                    last.then_inc(w.m_turned, 1)

                def project_k(b):
                    pe.wait_ge(w.c_copied, w.tiles(b))
                    for g in range(NG):
                        for t in range(DT):
                            last = pe.matmul(p_k[:, g * TK:(g + 1) * TK], wk_in[:, t, g * P:(g + 1) * P],
                                             cT[:, t, 0:TK], start=(t == 0), stop=(t == DT - 1))
                    last.then_inc(w.k_proj, 1)

                def project_q(b):
                    pe.wait_ge(w.m_copied, b.n + 1)
                    pe.wait_ge(w.x_copied, b.n + 1)
                    for g in range(NG):
                        parts = [(wl, xr, t) for wl, xr in ((wq_hi, x_hi), (wq_lo, x_hi), (wq_hi, x_lo))
                                 for t in range(DT)]
                        for n, (wl, xr, t) in enumerate(parts):
                            last = pe.matmul(p_q[:, g * S:(g + 1) * S], wl[:, t, g * P:(g + 1) * P], xr[:, t, :],
                                             start=(n == 0), stop=(n == len(parts) - 1))
                    last.then_inc(w.q_proj, 1)

                def project_v(b):
                    if b.from_(3):
                        pe.wait_ge(w.z, b.n - 2)
                    for k in range(w.TILES):
                        for t in range(DT):
                            last = pe.matmul(p_y[:, k * D:(k + 1) * D], cT[:, t, k * P:(k + 1) * P], wv_sb[:, t, :],
                                             start=(t == 0), stop=(t == DT - 1))
                    last.then_inc(w.v_proj, 1)

                def max_scores(b):
                    pe.wait_ge(w.m_copied, b.n + 1)
                    pe.wait_ge(w.q_rounded, b.n + 1)
                    pe.wait_ge(w.k_hi_spread, (b.n + 1) * KB)
                    if b.from_(1):
                        pe.wait_ge(w.exp[1], b.n * KB)
                    for kb in range(KB):
                        if kb:
                            pe.wait_ge(w.max_red, b.n * KB + kb)
                        n = w.blk(b, kb)
                        for q in range(QT):
                            for g in range(NG):
                                for half in range(2):
                                    c = (q * NG + g) * HG + half * HH
                                    last = pe.matmul(sc[:, c * BK:(c + HH) * BK],
                                                     q_mask[half][b.side][:, kb, g, q * P:(q + 1) * P],
                                                     k_hi[:, n, g, half * HH:(half + 1) * HH, :],
                                                     start=True, stop=True)
                            last.then_inc(w.max_mm[q], 1)

                def turn_max(b):
                    pe.wait_ge(w.neg_max, b.n + 1)
                    for q in range(QT):
                        last = pe.transpose(sc[:, q * P:(q + 1) * P], neg_max[:, q, :, :], ident[:, :])
                    last.then_inc(w.max_turned, 1)

                def scores(b, kb):
                    m, n = b.side, w.blk(b, kb)
                    if kb == 0:
                        pe.wait_ge(w.max_copied, b.n + 1)
                        pe.wait_ge(w.k_lo_spread, (b.n + 1) * KB)
                        pe.wait_ge(w.q_copied, 2 * b.n + 2)
                        pe.wait_ge(w.q_rest, b.n + 1)
                    else:
                        pe.wait_ge(w.exp[1], b.n * KB + kb)
                    for j in range(NP):
                        to = sc[:, j * S:(j + 1) * S]
                        g, c = j // (NP // NG), j % (NP // NG)
                        half = 2 * c // HH
                        hi, lo = (k[:, n, g, 2 * c:2 * c + 2, :] for k in (k_hi, k_lo))
                        pe.matmul(to, hi, q_mask[half][m][:, kb, g, :], start=True, stop=False)
                        pe.matmul(to, hi, q_rest[half][m][:, g, :], start=False, stop=False)
                        last = pe.matmul(to, lo, q_max[half][m][:, g, :], start=False, stop=True)
                        if j % (NP // 2) == NP // 2 - 1:
                            last.then_inc(w.score[j // (NP // 2)], 1)

                def weigh(b, kb):
                    if kb == 0:
                        pe.wait_ge(w.v_copied, w.tiles(b))
                        if (b + 1).exists(B):
                            pe.wait_ge(w.x_copied, b.n + 2)
                            if w.leads(b + 1):
                                pe.wait_ge(w.k_copied, w.tiles(b + 1))
                            elif b.from_(1):
                                pe.wait_ge(w.pv_copied, b.n)
                        else:
                            pe.wait_ge(w.pv_copied, B - 1)
                    v = b.ring if w.PB == 2 else b.side * ALL + kb
                    for g in range(NG):
                        pe.wait_ge(w.exp[g], b.n * KB + (kb + 1))
                        for to, left in ((p_x, None), (p_k, v_pair)):
                            for c in range(NP // NG):
                                j = g * (NP // NG) + c
                                last = pe.matmul(to[c * PQ:(c + 1) * PQ, g * S:(g + 1) * S],
                                                 ones_pair[:, :] if left is None else left[:, v, j, :],
                                                 probs[:, j, :], start=(kb == 0 and g == 0), stop=(kb == KB - 1),
                                                 skip_group_check=True)
                            if left is None and g == NG - 1 and kb == KB - 1:
                                last.then_inc(w.sums, 1)
                    last.then_inc(w.pv, 1)

                def out_project(b):
                    pe.wait_ge(w.attn, b.n + 1)
                    if (b + 2).exists(B):
                        pe.wait_ge(w.v_copied, w.tiles(b + 2))
                    for q in range(QT):
                        for g in range(NG):
                            last = pe.matmul(p_y[:, q * D:(q + 1) * D], attn[:, g * S + q * P:g * S + (q + 1) * P],
                                             wo_sb[:, g, :], start=(g == 0), stop=(g == NG - 1))
                    last.then_inc(w.out_mm, 1)

                def slot(i):
                    more = (i + 1).exists(B)
                    if more:
                        turn(i + 1)
                    if i.from_(2):
                        out_project(i - 2)
                    if more and w.leads(i + 1):
                        project_k(i + 1)
                    turn_max(i)
                    if more:
                        project_q(i + 1)
                    scores(i, 0)
                    if more and w.leads(i + 1):
                        project_v(i + 1)
                    weigh(i, 0)
                    for kb in range(1, KB):
                        scores(i, kb)
                        weigh(i, kb)
                    if more:
                        max_scores(i + 1)

                def first():
                    turn(Batch(0, 0))
                    for n in range(1, 3):
                        pe.wait_ge(s_weights[n], 16)
                    project_k(Batch(0, 0))
                    project_q(Batch(0, 0))
                    project_v(Batch(0, 0))

                def rest():
                    pe.wait_ge(s_const_k, max(KB, w.PB))
                    max_scores(Batch(0, 0))
                    slots(pe, slot)
                    out_project(Batch(0, B - 2))
                    pe.wait_ge(w.z, B - 1)
                    out_project(Batch(0, B - 1))

                return [first], rest

            (first,), rest = steps(last_block)
            first()
            pe.wait_ge(s_look, LOOKS + 1)
            pe.transpose(sc[0:1, 0:P], least_row[:, :], ident[:, :]).then_inc(s_look_turned, 1)
            pe.wait_ge(s_weights[3], 16)
            take_way(pe, steps, rest)


_INS = ['x', 'ctx_1024', 'mask_BxSxS2_bk1', 'L0_xattn_wq', 'L0_xattn_wk', 'L0_xattn_wv', 'L0_xattn_wo',
        'L0_xattn_gamma', 'L0_xattn_beta']


def kernel(**inputs):
    import numpy as np
    import concourse.bacc as bacc
    from concourse.bass_utils import run_bass_kernel_spmd

    nc = bacc.Bacc("TRN2", target_bir_lowering=False, num_devices=1)
    arrays, args = {}, []
    for name in _INS:
        a = np.ascontiguousarray(inputs[name])
        arrays[name] = a
        args.append(nc.dram_tensor(name, a.shape, mybir.dt.from_np(a.dtype), kind="ExternalInput").ap())
    shape = inputs['x'].shape
    out = nc.dram_tensor("out", shape, F32, kind="ExternalOutput").ap()
    build(nc, *args, out)
    r = run_bass_kernel_spmd(nc, [arrays], core_ids=[0])
    return r.results[0]["out"]
```
